# Optimizing a Trainium2 kernel written in Bass

```python
import numpy as np
import jax
import jax.numpy as jnp

def _softmax(x, axis=-1):
    return jax.nn.softmax(x, axis=axis)

def _gelu(x):
    return jax.nn.gelu(x, approximate=True)

def _silu(x):
    return jax.nn.silu(x)

def _sigmoid(x):
    return jax.nn.sigmoid(x)

def _layernorm(x, axis=-1, eps=1e-05):
    m = jnp.mean(x, axis=axis, keepdims=True)
    v = jnp.var(x, axis=axis, keepdims=True)
    return (x - m) / jnp.sqrt(v + eps)

def _scatter_add(tgt, idx, src, axis=0):
    return tgt.at[idx].add(src)

def _segment_sum(src, seg, n):
    return jax.ops.segment_sum(src, seg, n)
kernel_name = 'mk_gnn_preln_d1_gnn_r8_615f7c'

def setup_inputs(seed: int=0):
    np.random.seed(seed)
    _w = jnp.asarray

    def _rec_inputs():
        import jax
        import jax.numpy as jnp
        _gk = jax.random.key(seed)
        x = -0.0001126 + 1 * jax.random.normal(jax.random.fold_in(_gk, 1), (1250, 768), jnp.float32)
        src = jax.random.randint(jax.random.fold_in(_gk, 2), (20000,), 0, 1250, jnp.int32)
        dst = jnp.minimum((1250 * jax.random.uniform(jax.random.fold_in(_gk, 3), (20000,)) ** 2.0).astype(jnp.int32), 9999)
        _o = jnp.argsort(dst, stable=True)
        src = src[_o]
        dst = dst[_o]
        edge_type_34 = jax.random.randint(jax.random.fold_in(_gk, 12), (20000,), 0, 34, jnp.int32)
        return (x, src, dst, edge_type_34)
    x, src, dst, edge_type_34 = _rec_inputs()

    def _L0_gnn_setup():
        import jax, jax.numpy as jnp
        import numpy as np
        N_NODES = 1250
        N_EDGES = 12500
        N_REL = 34
        DIM = 768

        def _graph_encoder(x, edge_index, edge_type, W_rel, W_root, b_rgcn, W_gcn, b_gcn):
            n = x.shape[0]
            src, dst = (edge_index[0], edge_index[1])
            ones = jnp.ones((src.shape[0],), dtype=x.dtype)
            seg = edge_type * n + dst
            agg = jax.ops.segment_sum(x[src], seg, num_segments=N_REL * n)
            cnt = jax.ops.segment_sum(ones, seg, num_segments=N_REL * n)
            mean = agg.reshape(N_REL, n, -1) / jnp.maximum(cnt, 1.0).reshape(N_REL, n, 1)
            h1 = jnp.einsum('rni,rio->no', mean, W_rel) + x @ W_root + b_rgcn
            xw = h1 @ W_gcn
            deg = jax.ops.segment_sum(ones, dst, num_segments=n) + 1.0
            dinv = jax.lax.rsqrt(deg)
            norm = dinv[src] * dinv[dst]
            out = jax.ops.segment_sum(xw[src] * norm[:, None], dst, num_segments=n)
            out = out + xw * (dinv * dinv)[:, None]
            return out + b_gcn
        key = jax.random.key(seed)
        ks = jax.random.split(key, 6)
        scale = 1.0 / np.sqrt(DIM)
        x = jax.random.normal(ks[0], (N_NODES, DIM), dtype=jnp.float32)
        edge_index = jax.random.randint(ks[1], (2, N_EDGES), 0, N_NODES, dtype=jnp.int32)
        edge_type = jax.random.randint(ks[2], (N_EDGES,), 0, N_REL, dtype=jnp.int32)
        W_rel = jax.random.normal(ks[3], (N_REL, DIM, DIM), dtype=jnp.float32) * scale
        W_root = jax.random.normal(ks[4], (DIM, DIM), dtype=jnp.float32) * scale
        b_rgcn = jnp.zeros((DIM,), dtype=jnp.float32)
        W_gcn = jax.random.normal(ks[5], (DIM, DIM), dtype=jnp.float32) * scale
        b_gcn = jnp.zeros((DIM,), dtype=jnp.float32)
        return {'x': x, 'edge_index': edge_index, 'edge_type': edge_type, 'W_rel': W_rel, 'W_root': W_root, 'b_rgcn': b_rgcn, 'W_gcn': W_gcn, 'b_gcn': b_gcn}
    _L0_gnn_all = _L0_gnn_setup()
    _L0_gnn_in = {k: v for k, v in _L0_gnn_all.items() if k in ('W_rel', 'W_root', 'b_rgcn', 'W_gcn', 'b_gcn')}
    del _L0_gnn_all
    return {'x': x, 'src': src, 'dst': dst, 'edge_type_34': edge_type_34, 'L0_gnn_W_rel': _L0_gnn_in['W_rel'], 'L0_gnn_W_root': _L0_gnn_in['W_root'], 'L0_gnn_b_rgcn': _L0_gnn_in['b_rgcn'], 'L0_gnn_W_gcn': _L0_gnn_in['W_gcn'], 'L0_gnn_b_gcn': _L0_gnn_in['b_gcn']}

def reference(x, src, dst, edge_type_34, L0_gnn_W_rel, L0_gnn_W_root, L0_gnn_b_rgcn, L0_gnn_W_gcn, L0_gnn_b_gcn):
    import jax
    import jax.numpy as jnp

    def _L0_gnn_ref(x, edge_index, edge_type, W_rel, W_root, b_rgcn, W_gcn, b_gcn):
        import jax, jax.numpy as jnp
        import numpy as np
        N_NODES = 1250
        N_EDGES = 12500
        N_REL = 34
        DIM = 768

        def _graph_encoder(x, edge_index, edge_type, W_rel, W_root, b_rgcn, W_gcn, b_gcn):
            n = x.shape[0]
            src, dst = (edge_index[0], edge_index[1])
            ones = jnp.ones((src.shape[0],), dtype=x.dtype)
            seg = edge_type * n + dst
            agg = jax.ops.segment_sum(x[src], seg, num_segments=N_REL * n)
            cnt = jax.ops.segment_sum(ones, seg, num_segments=N_REL * n)
            mean = agg.reshape(N_REL, n, -1) / jnp.maximum(cnt, 1.0).reshape(N_REL, n, 1)
            h1 = jnp.einsum('rni,rio->no', mean, W_rel) + x @ W_root + b_rgcn
            xw = h1 @ W_gcn
            deg = jax.ops.segment_sum(ones, dst, num_segments=n) + 1.0
            dinv = jax.lax.rsqrt(deg)
            norm = dinv[src] * dinv[dst]
            out = jax.ops.segment_sum(xw[src] * norm[:, None], dst, num_segments=n)
            out = out + xw * (dinv * dinv)[:, None]
            return out + b_gcn
        return _graph_encoder(x, edge_index, edge_type, W_rel, W_root, b_rgcn, W_gcn, b_gcn)
    edge_index = jnp.stack([src, dst])
    h = jnp.maximum(_layernorm(x, axis=-1), 0.0)
    x = x + _L0_gnn_ref(h, edge_index, edge_type_34, L0_gnn_W_rel, L0_gnn_W_root, L0_gnn_b_rgcn, L0_gnn_W_gcn, L0_gnn_b_gcn)
    return x

_drawn_inputs = setup_inputs


def setup_inputs(seed=0):
    import zlib

    import numpy as np

    out = dict(_drawn_inputs(seed))
    spreads = {'L0_gnn_b_rgcn': (0.0, 0.1), 'L0_gnn_b_gcn': (0.0, 0.1)}
    factors = {}
    for name, (base, spread) in spreads.items():
        noise = np.random.default_rng([zlib.crc32(name.encode()), seed]).standard_normal(out[name].shape)
        drawn = base * np.exp(spread * noise) if base else spread * noise
        out[name] = jnp.asarray(drawn.astype(out[name].dtype))
    for name, factor in factors.items():
        out[name] = (out[name] * factor).astype(out[name].dtype)
    return out
```

```python
import concourse.bass as bass
from concourse import mybir
from contextlib import ExitStack


def relational_gnn_kernel(
    nc: bass.Bass,
    x: bass.AP,
    src: bass.AP,
    dst: bass.AP,
    edge_type: bass.AP,
    W_rel: bass.AP,
    W_root: bass.AP,
    b_rgcn: bass.AP,
    W_gcn: bass.AP,
    b_gcn: bass.AP,
    out: bass.AP,
):
    f32, f32r, f16, i32 = mybir.dt.float32, mybir.dt.float32r, mybir.dt.float16, mybir.dt.int32
    ALU = mybir.AluOpType
    ACT = mybir.ActivationFunctionType
    AX = mybir.AxisListType

    P = 128
    N, D = x.shape
    E = src.shape[0]
    R = W_rel.shape[0]
    ND, NB = 125, 10
    EP, ET = 125, 160
    assert ND * NB == N and EP * ET == E
    KC = D // P
    HALF = D // 2
    BANK = 512
    G = R + NB
    MSG_TILES = (E + R * P) // P
    U = 6
    AGG_TILES = -(-((E + NB * (P - 1)) // P) // U) * U
    TW = 192
    assert MSG_TILES % 2 == 0 and max(MSG_TILES, AGG_TILES) < TW
    LAYERS = R + 2
    WN = KC * D
    EPS = 1e-5
    SURE_PAIRS = ET // 2
    assert 2 * SURE_PAIRS <= MSG_TILES and ET % 2 == 0
    REL, FIRST, WSLOT, BLK, USED, TOTAL = range(6)

    h_dram = nc.dram_tensor("h_rows", (N, D), f32, kind="Internal").ap()
    msg_dram = nc.dram_tensor("message_rows", (MSG_TILES * P, D), f32, kind="Internal").ap()
    inv_dram = nc.dram_tensor("inverse_counts", (N * R, 1), f32, kind="Internal").ap()
    xw_dram = nc.dram_tensor("xw_rows", (N, D), f32, kind="Internal").ap()

    def nodes(ap):
        return ap.rearrange("(b d) f -> d b f", b=NB)

    def weights(ap):
        return ap.rearrange("(c p) n -> p c n", c=KC)

    with ExitStack() as ctx:
        def sb(name, shape, dt):
            return ctx.enter_context(nc.sbuf_tensor(name, shape, dt))

        def sem(name):
            return ctx.enter_context(nc.semaphore(name))

        ring_at = -(-nc.sbuf_base // 32) * 32
        sb("ring_memory", [P, 4 * WN], f32)
        at = [ring_at, ring_at + 8 * WN]

        def placed(slot, name, shape, dt, size):
            here = at[slot]
            at[slot] += -(-size // 32) * 32
            assert at[slot] <= ring_at + (slot + 1) * 8 * WN
            return nc.alloc_sbuf_tensor_at(name, shape, dt, offset=here)

        wr = nc.alloc_sbuf_tensor_at("w_ring", [P, 2, 2, KC, D], f32r, offset=ring_at)
        wraw = sb("w_raw", [P, KC, D], f32)
        rows6 = wraw
        xt = sb("x_nodes", [ND, NB, D], f32)
        acc = sb("acc", [ND, NB, D], f32)
        rows = [sb(f"h_gathered{u}", [P, D], f32) for u in range(2)]
        ahi = [sb(f"a_hi{u}", [P, KC, P], f32r) for u in range(2)]
        alo = [sb(f"a_lo{u}", [P, KC, P], f32r) for u in range(2)]
        ysb = [sb(f"y_out{u}", [P, D], f32) for u in range(2)]
        idx_src = sb("idx_src", [P, TW], i32)
        idx_cell = sb("idx_cell", [P, TW], i32)
        idx_msg = sb("idx_msg", [P, TW], i32)
        idx_xw = sb("idx_xw", [P, TW], i32)
        dloc = sb("dst_local", [P, TW], f32)
        ctrl = sb("ctrl", [1, 6, TW], i32)
        dinv = sb("dinv", [ND, NB], f32)
        ident = sb("identity", [P, P], f32)
        iota_i = sb("iota_i", [P, R * NB], i32)
        iota_f = sb("iota_f", [P, TW], f32)
        iota_h = sb("iota_h", [P, R * NB], f16)
        part_i = sb("part_i", [P, 1], i32)
        part_f = sb("part_f", [P, 1], f32)
        idxbuf = [sb(f"idxbuf{u}", [P, 1], i32) for u in range(U)]
        cellbuf = [sb(f"cellbuf{u}", [P, 1], i32) for u in range(2)]
        invbuf = [sb(f"invbuf{u}", [P, 1], f32) for u in range(2)]
        selector = [sb(f"selector{u}", [P, P], f32) for u in range(2)]

        psT = [ctx.enter_context(nc.psum_tensor(f"psT{u}", [P, 2 * BANK], f32)) for u in range(2)]
        psY = [ctx.enter_context(nc.psum_tensor(f"psY{u}", [P, 2 * BANK], f32)) for u in range(2)]

        def tview(u, m):
            return psT[u][:, 0:D].rearrange("p (c m) -> p c m", c=KC)[:, :, 0:m]

        def yview(u, m):
            return psY[u][0:m, :].rearrange("p (h n) -> p h n", h=2)[:, :, 0:HALF]

        def halves(ap):
            return ap.rearrange("p (h n) -> p h n", h=2)

        s_edges, s_x, s_bias = sem("edges_loaded"), sem("x_loaded"), sem("bias_loaded")
        s_iota = sem("iota_made")
        s_dve = sem("vector_step")
        s_zero, s_fill = sem("zero_rows_made"), sem("zero_rows_stored")
        s_stats, s_std, s_norm = sem("stats_ready"), sem("std_ready"), sem("norm_ready")
        s_h, s_hst = sem("h_ready"), sem("h_stored")
        s_wload, s_whi, s_wlo = sem("w_loaded"), sem("w_hi_ready"), sem("w_lo_ready")
        s_dT, s_dhi, s_dlo = sem("dense_transposed"), sem("dense_hi"), sem("dense_lo")
        s_dprod, s_dev = sem("dense_product"), sem("dense_evacuated")
        s_sm_in, s_sm = sem("small_operand"), sem("small_product")
        s_hot, s_tab = sem("onehots_ready"), sem("onehots_used")
        s_hot2, s_tab2 = sem("dst_onehots_ready"), sem("dst_onehots_used")
        s_tables2 = sem("dst_tables_ready")
        s_inv, s_invst = sem("inverse_ready"), sem("inverse_stored")
        s_deg, s_sdeg = sem("degree_ready"), sem("sqrt_degree_ready")
        s_tables = sem("tables_ready")
        s_rowi, s_celli = sem("row_index_copied"), sem("cell_index_copied")
        s_xb = sem("x_plus_bias")
        s_rows = [sem(f"rows_gathered{u}") for u in range(2)]
        s_invg = [sem(f"inverse_gathered{u}") for u in range(2)]
        s_T, s_hi, s_lo = sem("tile_transposed"), sem("tile_hi"), sem("tile_lo")
        s_prod, s_evac = sem("tile_product"), sem("tile_evacuated")
        s_yst = [sem(f"messages_stored{u}") for u in range(2)]
        s_g6 = [[sem(f"agg{ph}_gathered{u}") for u in range(U)] for ph in range(2)]
        s_ai = [sem(f"agg{ph}_index") for ph in range(2)]
        s_sel = [sem(f"agg{ph}_selector") for ph in range(2)]
        s_ap = [sem(f"agg{ph}_product") for ph in range(2)]
        s_aa = [sem(f"agg{ph}_added") for ph in range(2)]
        s_h1 = sem("h1_complete")
        s_passed = sem("waits_passed")
        s_xw, s_xwst = sem("xw_ready"), sem("xw_stored")
        s_fin, s_out = sem("out_ready"), sem("out_stored")

        prep = ctx.enter_context(ExitStack())

        def tmp(name, shape, dt):
            return prep.enter_context(nc.sbuf_tensor(name, shape, dt))

        edges_i = placed(1, "edges_i", [EP, 3, ET], i32, 12 * ET)
        hot = placed(1, "group_onehot", [EP, G, ET], f32, 4 * G * ET)
        src_f, dst_f, rel_f, blk_f, dp1_f, cell_f = (
            placed(1, name, [EP, ET], f32, 4 * ET) for name in ("src_f", "dst_f", "rel_f", "blk_f", "dp1_f", "cell_f"))
        scan = placed(0, "group_scan", [EP, G * ET], f32, 4 * G * ET)
        pos_f = placed(0, "pos_f", [EP, 2, ET], f32, 8 * ET)
        pos_i = placed(0, "pos_i", [EP, 2, ET], i32, 8 * ET)
        lo_i = pos_f[:, :, :].bitcast(i32)
        lo_f = tmp("lo_f", [EP, 2, ET], f32)
        hi_f = tmp("hi_f", [EP, 2, ET], f32)
        edge_v = tmp("edge_values", [EP, 3, ET], f32)
        tot = tmp("totals", [EP, G], f32)
        tots = tmp("totals_scan", [EP, G], f32)
        delta = tmp("delta", [EP, G], f32)
        savec = tmp("first_column", [EP, G], f32)
        tri = tmp("tri", [P, P], f32)
        ones = tmp("ones", [P, P], f32)
        c128 = tmp("c128", [P, P], f32)
        mcol = tmp("mask_columns", [P, 8], f32)
        masks = tmp("masks", [G, 3, P], f32)
        ncol = tmp("group_sizes", [G, 4], f32)
        ncol_i = tmp("group_sizes_i", [G, 2], i32)
        tri_t = tmp("tri_tiles", [G, G], f32)
        cmpt = tmp("starts_compared", [G, 2, TW], f32)
        rel_t = tmp("rel_of_tile", [P, TW], f32)
        stats = tmp("bn_stats", [ND, 2, 6], f32)
        mv = tmp("mean_var", [ND, NB, 2], f32)
        nrm = tmp("norm", [ND, 3, NB], f32)
        brow, bgcn = ysb[0][0:ND, :], ysb[1][0:ND, :]
        oh_lo1 = [placed(0, f"oh_lo1{u}", [EP, P], f32, 4 * P) for u in range(2)]
        oh_m1 = [placed(0, f"oh_m1{u}", [EP, MSG_TILES], f32, 4 * MSG_TILES) for u in range(2)]
        oh_d = [placed(0, f"oh_d{u}", [EP, P], f16, 2 * P) for u in range(2)]
        oh_c = [placed(0, f"oh_c{u}", [EP, NB * R], f16, 2 * NB * R) for u in range(2)]
        oh_lo2 = [tmp(f"oh_lo2{u}", [EP, P], f32) for u in range(2)]
        oh_m2 = [tmp(f"oh_m2{u}", [EP, 2, AGG_TILES], f32) for u in range(2)]
        word = tmp("table_words", [P, 2, TW], i32)
        cnt = tmp("cell_counts", [ND, NB, R], f32)
        inv = tmp("inverse", [ND, NB, R], f32)
        deg = tmp("degree", [ND, 3, NB], f32)

        block = ctx.enter_context(nc.Block())

        def static_view(t):
            return t[:, :, :].rearrange("p c n -> p (c n)")

        def first_pair(j):
            return isinstance(j, int) and j == 0

        def every_pair(eng, pair, between=None):
            pair(0)
            with eng.Fori(1, SURE_PAIRS) as j:
                pair(j)
            if between:
                between()
            with eng.Fori(SURE_PAIRS, MSG_TILES // 2) as j:
                used = eng.value_load(ctrl[0:1, USED, bass.ds(2 * j, 1)], min_val=0, max_val=1)
                with eng.If(used == 1):
                    pair(j)

        def tiles_done(eng):
            return eng.value_load(ctrl[0:1, TOTAL, 0:1], min_val=2 * SURE_PAIRS, max_val=MSG_TILES)

        @block.sync
        def _(sp):
            for n, a in enumerate((src, dst, edge_type)):
                sp.dma_start(edges_i[:, n, :], a.rearrange("(p t) -> p t", p=EP)).then_inc(s_edges, 16)
            sp.dma_start(xt[:, :, :], nodes(x)).then_inc(s_x, 16)
            sp.dma_start(wraw[:, :, :], weights(W_root)).then_inc(s_wload, 16)
            sp.dma_start(brow, b_rgcn.partition_broadcast(ND)).then_inc(s_bias, 16)
            sp.dma_start(bgcn, b_gcn.partition_broadcast(ND)).then_inc(s_bias, 16)
            spare = MSG_TILES - 2 * SURE_PAIRS
            sp.wait_ge(s_zero, 1)
            sp.dma_start(msg_dram[2 * SURE_PAIRS * P:, :].rearrange("(t p) d -> p t d", p=P),
                         rows[0][:, :].unsqueeze(1).broadcast_to((P, spare, D))).then_inc(s_fill, 16)
            sp.wait_ge(s_h, NB)
            sp.dma_start(nodes(h_dram), acc[:, :, :]).then_inc(s_hst, 16)
            with sp.Fori(0, R) as r:
                sp.wait_ge(s_wlo, r + 1)
                sp.wait_ge(s_whi, r + 1)
                sp.dma_start(wraw[:, :, :],
                             W_rel[bass.ds(r, 1), :, :].rearrange("o (c p) n -> p (o c) n", c=KC)
                             ).then_inc(s_wload, 16)
            sp.wait_ge(s_wlo, R + 1)
            sp.wait_ge(s_whi, R + 1)
            sp.dma_start(wraw[:, :, :], weights(W_gcn)).then_inc(s_wload, 16)
            sp.wait_ge(s_xw, NB)
            sp.dma_start(nodes(xw_dram), acc[:, :, :]).then_inc(s_xwst, 16)
            for b in range(NB):
                sp.wait_ge(s_fin, b + 1)
                sp.dma_start(out[b * ND:(b + 1) * ND, :], xt[:, b, :]).then_inc(s_out, 16)
            sp.wait_ge(s_out, 16 * NB)

        @block.gpsimd
        def _(pool):
            nc.gpsimd.iota(iota_i[:, :], [[1, R * NB]], base=0, channel_multiplier=0).then_inc(s_iota, 1)
            nc.gpsimd.iota(part_i[:, :], [[0, 1]], base=0, channel_multiplier=1).then_inc(s_iota, 1)

            nc.gpsimd.memset(rows[0][:, :], 0.0).then_inc(s_zero, 1)

            pool.wait_ge(s_bias, 32)
            pool.wait_ge(s_h, NB)
            for b in range(NB):
                nc.gpsimd.tensor_tensor(xt[:, b, :], xt[:, b, :], bgcn, ALU.add).then_inc(s_xb, 1)

            pool.wait_ge(s_tables, 1)
            pool.wait_ge(s_fill, 16)
            pool.wait_ge(s_hst, 16)
            pool.wait_ge(s_invst, 16)

            def gather_h(t, u):
                nc.gpsimd.tensor_copy(idxbuf[u][:, :], idx_src[:, bass.ds(t, 1)]).then_inc(s_rowi, 1)
                pool.wait_ge(s_rowi, t + 1)
                pool.sem_inc(s_passed)
                nc.gpsimd.indirect_dma_start(
                    rows[u][:, :], None, h_dram,
                    bass.IndirectOffsetOnAxis(idxbuf[u][:, 0:1], 0)).then_inc(s_rows[u], 16)

            def gather_inverse(t, u):
                nc.gpsimd.tensor_copy(cellbuf[u][:, :], idx_cell[:, bass.ds(t, 1)]).then_inc(s_celli, 1)
                pool.wait_ge(s_celli, t + 1)
                pool.sem_inc(s_passed)
                nc.gpsimd.indirect_dma_start(
                    invbuf[u][:, :], None, inv_dram,
                    bass.IndirectOffsetOnAxis(cellbuf[u][:, 0:1], 0)).then_inc(s_invg[u], 16)

            def pair(j):
                for u in range(2):
                    pool.wait_ge(s_T, 2 * j + (u + 1))
                    gather_h(2 * j + (u + 2), u)
                    if not first_pair(j):
                        pool.wait_ge(s_evac, 2 * j + (u - 1))
                        pool.sem_inc(s_passed)
                    gather_inverse(2 * j + u, u)

            for u in range(2):
                gather_h(u, u)
            every_pair(pool, pair)

            def gather_rows(ph, w, u, index, table):
                nc.gpsimd.tensor_copy(idxbuf[u][:, :], index[:, bass.ds(w, 1)]).then_inc(s_ai[ph], 1)
                pool.wait_ge(s_ai[ph], w + 1)
                pool.sem_inc(s_passed)
                nc.gpsimd.indirect_dma_start(
                    rows6[:, u, :], None, table,
                    bass.IndirectOffsetOnAxis(idxbuf[u][:, 0:1], 0)).then_inc(s_g6[ph][u], 16)

            for ph, index, table in ((0, idx_msg, msg_dram), (1, idx_xw, xw_dram)):
                if ph == 0:
                    pool.wait_ge(s_tables2, 1)
                    for u in range(2):
                        pool.wait_ge(s_yst[u], tiles_done(pool) * 8)
                        pool.sem_inc(s_passed)
                    pool.wait_ge(s_whi, LAYERS)
                    pool.wait_ge(s_wlo, LAYERS)
                else:
                    pool.wait_ge(s_xwst, 16)
                for u in range(U):
                    gather_rows(ph, u, u, index, table)
                with pool.Fori(1, AGG_TILES // U) as j:
                    for u in range(U):
                        pool.wait_ge(s_ap[ph], U * j + (u - U + 1))
                        gather_rows(ph, U * j + u, u, index, table)

        @block.scalar
        def _(act):
            act.wait_ge(s_stats, 1)
            nc.scalar.activation(nrm[:, 0, :], nrm[:, 1, :], ACT.Sqrt).then_inc(s_std, 1)
            act.wait_ge(s_norm, 1)
            act.wait_ge(s_x, 16)
            for b in range(NB):
                nc.scalar.activation(acc[:, b, :], xt[:, b, :], ACT.Relu, bias=nrm[:, 2, b:b + 1],
                                     scale=nrm[:, 1, b:b + 1]).then_inc(s_h, 1)
            act.wait_ge(s_wload, 16)
            nc.scalar.copy(wr[:, 0, 0, :, :], wraw[:, :, :]).then_inc(s_whi, 1)

            def dense_hi(b, n):
                act.wait_ge(s_dT, n + 1)
                if n >= 2:
                    act.wait_ge(s_dprod, n - 1)
                nc.scalar.copy(ahi[b % 2][:, :, 0:ND], tview(b % 2, ND)).then_inc(s_dhi, 1)

            for b in range(NB):
                dense_hi(b, b)
            act.wait_ge(s_deg, 1)
            nc.scalar.activation(deg[:, 1, :], deg[:, 0, :], ACT.Sqrt).then_inc(s_sdeg, 1)
            act.wait_ge(s_inv, 1)
            act.dma_start(inv_dram.rearrange("(b d r) o -> d b (r o)", b=NB, r=R),
                          inv[:, :, :]).then_inc(s_invst, 16)
            act.wait_ge(s_wload, 32)
            nc.scalar.copy(wr[:, 1, 0, :, :], wraw[:, :, :]).then_inc(s_whi, 1)
            act.wait_ge(s_tables, 1)

            def tile_hi(t, u):
                act.wait_ge(s_T, t + 1)
                nc.scalar.copy(ahi[u][:, :, :], tview(0, P)).then_inc(s_hi, 1)

            def split_next_hi(t, very_first):
                first = act.value_load(ctrl[0:1, FIRST, bass.ds(t, 1)], min_val=0, max_val=1)
                rel = act.value_load(ctrl[0:1, REL, bass.ds(t, 1)], min_val=0, max_val=R - 1)
                slot = act.value_load(ctrl[0:1, WSLOT, bass.ds(t, 1)], min_val=0, max_val=1)
                with act.If(first == 1):
                    if not very_first:
                        act.wait_ge(s_prod, t)
                    act.wait_ge(s_wload, rel * 16 + 48)
                    nc.scalar.copy(wr[:, bass.ds(1 - slot, 1), 0, :, :].rearrange("p o c n -> p (o c) n"),
                                   wraw[:, :, :]).then_inc(s_whi, 1)

            def tile_out(t, u, j):
                act.wait_ge(s_prod, t + 1)
                act.wait_ge(s_invg[u], 16 * j + 16)
                if not first_pair(j):
                    act.wait_ge(s_yst[u], 16 * j)
                nc.scalar.activation(halves(ysb[u][:, :]), yview(u, P), ACT.Copy,
                                     scale=invbuf[u][:, 0:1]).then_inc(s_evac, 1)
                act.wait_ge(s_evac, t + 1)
                act.dma_start(msg_dram[bass.ds(t * P, P), :], ysb[u][:, :]).then_inc(s_yst[u], 16)

            def pair(j):
                for u in range(2):
                    if not (first_pair(j) and u == 0):
                        act.wait_ge(s_prod, 2 * j + u)
                    tile_hi(2 * j + (u + 1), 1 - u)
                    split_next_hi(2 * j + u, first_pair(j) and u == 0)
                    tile_out(2 * j + u, u, j)

            tile_hi(0, 0)
            every_pair(act, pair)

            def gcn_out(b):
                act.wait_ge(s_dprod, NB + b + 1)
                nc.scalar.activation(halves(acc[:, b, :]), yview(b % 2, ND), ACT.Copy,
                                     scale=dinv[:, b:b + 1]).then_inc(s_xw, 1)

            for b in range(NB):
                dense_hi(b, NB + b)
                if b:
                    gcn_out(b - 1)
            gcn_out(NB - 1)

        @block.vector
        def _(dve):
            chain = [0]
            V = nc.vector

            def step(ins):
                chain[0] += 1
                ins.then_inc(s_dve, 1)
                dve.wait_ge(s_dve, chain[0])

            def inverse_sqrt(y, v, root, t):
                step(V.reciprocal(root, root))
                step(V.tensor_tensor(t, root, root, ALU.mult))
                step(V.scalar_tensor_tensor(t, t, -0.5, v, ALU.mult, ALU.mult))
                step(V.tensor_scalar(t, t, 1.5, None, ALU.add))
                step(V.tensor_tensor(y, root, t, ALU.mult))

            dve.wait_ge(s_x, 16)
            for b in range(NB):
                V.bn_stats(stats[:, 0, :], xt[:, b, 0:HALF])
                step(V.bn_stats(stats[:, 1, :], xt[:, b, HALF:D]))
                step(V.bn_aggr(mv[:, b, :], stats[:, :, :].rearrange("p a b -> p (a b)")))
            V.tensor_scalar(nrm[:, 1, :], mv[:, :, 1], EPS, None, ALU.add).then_inc(s_stats, 1)
            dve.wait_ge(s_std, 1)
            inverse_sqrt(nrm[:, 1, :], nrm[:, 1, :], nrm[:, 0, :], nrm[:, 2, :])
            V.scalar_tensor_tensor(nrm[:, 2, :], mv[:, :, 0], -1.0, nrm[:, 1, :],
                                   ALU.mult, ALU.mult).then_inc(s_norm, 1)

            dve.wait_ge(s_iota, 2)
            V.tensor_copy(part_f[:, :], part_i[:, :])
            V.tensor_copy(iota_h[:, :], iota_i[:, :])
            V.memset(ones[:, :], 1.0)
            V.memset(c128[:, :], float(P))
            step(V.tensor_copy(iota_f[:, :], iota_i[:, 0:TW]))
            V.tensor_scalar(tri[:, :], iota_f[:, 0:P], part_f[:, 0:1], None, ALU.is_gt)
            V.tensor_scalar(mcol[:, 0:1], part_f[:, :], 1.0, None, ALU.is_ge)
            V.tensor_scalar(mcol[:, 1:2], part_f[:, :], float(R), None, ALU.is_lt)
            V.tensor_scalar(mcol[:, 2:3], part_f[:, :], float(R + 1), None, ALU.is_ge)
            step(V.tensor_scalar(ident[:, :], iota_f[:, 0:P], part_f[:, 0:1], None, ALU.is_equal))
            V.tensor_scalar(masks[:, 0, :], ones[0:G, :], mcol[0:G, 0:1], mcol[0:G, 1:2], ALU.mult, ALU.mult)
            V.tensor_scalar(masks[:, 1, :], ones[0:G, :], mcol[0:G, 1:2], None, ALU.mult)
            step(V.tensor_scalar(masks[:, 2, :], ones[0:G, :], mcol[0:G, 2:3], None, ALU.mult))

            def dense_lo(b, n):
                dve.wait_ge(s_dhi, n + 1)
                V.tensor_tensor(alo[b % 2][:, :, 0:ND], tview(b % 2, ND), ahi[b % 2][:, :, 0:ND].bitcast(f32),
                                ALU.subtract).then_inc(s_dlo, 1)

            def split_lo(slot):
                return V.tensor_tensor(wr[:, slot, 1, :, :], wraw[:, :, :],
                                       wr[:, slot, 0, :, :].bitcast(f32), ALU.subtract)

            def edges_to_float():
                dve.wait_ge(s_edges, 48)
                V.tensor_copy(src_f[:, :], edges_i[:, 0, :])
                V.tensor_copy(dst_f[:, :], edges_i[:, 1, :])
                step(V.tensor_copy(rel_f[:, :], edges_i[:, 2, :]))

            def node_block():
                step(V.tensor_scalar(blk_f[:, :], dst_f[:, :], float(ND), None, ALU.is_ge))
                for k in range(2, NB):
                    step(V.scalar_tensor_tensor(blk_f[:, :], dst_f[:, :], float(k * ND), blk_f[:, :],
                                                ALU.is_ge, ALU.add))
                step(V.scalar_tensor_tensor(dp1_f[:, :], blk_f[:, :], -float(ND), dst_f[:, :],
                                            ALU.mult, ALU.add))
                V.scalar_tensor_tensor(cell_f[:, :], blk_f[:, :], float(R), rel_f[:, :], ALU.mult, ALU.add)
                step(V.tensor_scalar(dp1_f[:, :], dp1_f[:, :], 1.0, None, ALU.add))

            def relation_onehot():
                step(V.tensor_tensor(hot[:, 0:R, :], rel_f[:, :].unsqueeze(1).broadcast_to((EP, R, ET)),
                                     iota_f[0:EP, 0:R].unsqueeze(2).broadcast_to((EP, R, ET)), ALU.is_equal))

            def block_onehot():
                step(V.tensor_tensor(hot[:, R:G, :], blk_f[:, :].unsqueeze(1).broadcast_to((EP, NB, ET)),
                                     iota_f[0:EP, 0:NB].unsqueeze(2).broadcast_to((EP, NB, ET)), ALU.is_equal))

            def totals():
                step(V.tensor_reduce(tot[:, :], hot[:, :, :], AX.X, ALU.add))
                step(V.tensor_tensor_scan(tots[:, :], tot[:, :], tot[:, :], 0.0, ALU.add, ALU.max))

            dve.wait_ge(s_whi, 1)
            split_lo(0).then_inc(s_wlo, 1)
            dve.wait_ge(s_bias, 32)
            between = [edges_to_float, node_block, relation_onehot, block_onehot, totals]

            def root_out(b):
                dve.wait_ge(s_dprod, b + 1)
                dve.wait_ge(s_hst, 16)
                V.tensor_tensor(halves(acc[:, b, :]), yview(b % 2, ND), halves(brow),
                                ALU.add).then_inc(s_dev, 1)

            for b in range(NB):
                dense_lo(b, b)
                if b:
                    root_out(b - 1)
                if between:
                    between.pop(0)()
            root_out(NB - 1)

            V.tensor_copy(tri_t[:, :], tri[0:G, 0:G]).then_inc(s_sm_in, 1)
            dve.wait_ge(s_sm, 1)
            step(V.tensor_scalar(ncol[:, 0:1], psY[0][0:G, 0:1], float(P - 1), None, ALU.add))
            step(V.tensor_copy(ncol_i[:, 0:1], ncol[:, 0:1]))
            step(V.tensor_scalar(ncol_i[:, 1:2], ncol_i[:, 0:1], 7, None, ALU.arith_shift_right))
            step(V.tensor_copy(ncol[:, 1:2], ncol_i[:, 1:2]))
            step(V.tensor_scalar(ncol[:, 2:3], ncol[:, 1:2], mcol[0:G, 1:2], None, ALU.max))
            step(V.tensor_scalar(tri_t[:, 0:R], tri_t[:, 0:R], ncol[:, 2:3], None, ALU.mult))
            step(V.tensor_scalar(tri_t[:, R:G], tri_t[:, R:G], ncol[:, 2:3], masks[:, 2, 0:1],
                                 ALU.mult, ALU.mult))
            step(V.tensor_scalar(mcol[0:G, 3:4], part_f[0:G, :], float(R), None, ALU.is_equal))
            step(V.tensor_scalar(mcol[0:G, 4:5], ncol[:, 2:3], mcol[0:G, 3:4], None, ALU.mult))
            V.scalar_tensor_tensor(tri_t[:, R:G], tri[0:G, R:G], mcol[0:G, 4:5], tri_t[:, R:G],
                                   ALU.mult, ALU.add).then_inc(s_sm_in, 1)
            dve.wait_ge(s_sm, 2)
            step(V.tensor_tensor(delta[:, :], psY[1][0:EP, 8:8 + G], tots[:, :], ALU.subtract))
            step(V.tensor_tensor(delta[:, :], delta[:, :], tot[:, :], ALU.add))
            step(V.tensor_copy(savec[:, :], hot[:, :, 0]))
            V.tensor_tensor(hot[:, 0:1, 0], savec[:, 0:1], delta[:, 0:1], ALU.add)
            step(V.tensor_tensor(hot[:, 1:G, 0], savec[:, 1:G], delta[:, 1:G], ALU.add))
            step(V.tensor_tensor(hot[:, 1:G, 0], hot[:, 1:G, 0], delta[:, 0:G - 1], ALU.subtract))
            hot2 = hot[:, :, :].rearrange("p g t -> p (g t)")
            step(V.tensor_tensor_scan(scan[:, :], hot2, hot2, 0.0, ALU.add, ALU.bypass))
            step(V.tensor_copy(hot[:, :, 0], savec[:, :]))
            step(V.tensor_tensor(scan[:, :], scan[:, :], hot2, ALU.mult))
            scan3 = scan[:, :].rearrange("p (g t) -> p t g", g=G)
            V.tensor_reduce(pos_f[:, 0, :], scan3[:, :, 0:R], AX.X, ALU.add)
            step(V.tensor_reduce(pos_f[:, 1, :], scan3[:, :, R:G], AX.X, ALU.add))
            step(V.tensor_scalar(pos_i[:, :, :], pos_f[:, :, :], -1.0, None, ALU.add))
            step(V.tensor_scalar(lo_i, pos_i[:, :, :], P - 1, None, ALU.bitwise_and))
            step(V.tensor_scalar(pos_i[:, :, :], pos_i[:, :, :], 7, None, ALU.arith_shift_right))
            V.tensor_copy(lo_f[:, :, :], lo_i)
            step(V.tensor_copy(hi_f[:, :, :], pos_i[:, :, :]))
            dve.wait_ge(s_sm, 3)
            step(V.tensor_copy(ncol[:, 3:4], psY[1][0:G, BANK:BANK + 1]))
            V.tensor_scalar(cmpt[:, 0, :], iota_f[0:G, :], ncol[:, 3:4], None, ALU.is_ge)
            V.tensor_scalar(cmpt[:, 1, :], iota_f[0:G, :], ncol[:, 3:4], None,
                            ALU.is_equal).then_inc(s_sm_in, 1)
            dve.wait_ge(s_sm, 7)
            V.tensor_copy(ctrl[0:1, REL, :], psY[0][0:1, 64:64 + TW])
            V.tensor_copy(ctrl[0:1, FIRST, :], psY[0][0:1, BANK:BANK + TW])
            V.tensor_copy(ctrl[0:1, BLK, :], psY[1][0:1, BANK:BANK + TW])
            V.tensor_copy(rel_t[:, :], psY[0][:, 64:64 + TW])
            step(V.tensor_copy(ncol[0:1, 0:1], psY[1][0:1, BANK + TW:BANK + TW + 1]))
            V.tensor_scalar(ctrl[0:1, USED, :], iota_f[0:1, :], ncol[0:1, 0:1], None, ALU.is_lt)
            step(V.tensor_scalar(ctrl[0:1, TOTAL, 0:1], ncol[0:1, 0:1], 1.0, float(2 * SURE_PAIRS),
                                 ALU.add, ALU.max))
            step(V.tensor_scalar(ctrl[0:1, TOTAL, 0:1], ctrl[0:1, TOTAL, 0:1], 1, 1,
                                 ALU.arith_shift_right, ALU.logical_shift_left))
            step(V.tensor_scalar(ctrl[0:1, WSLOT, :], psY[0][0:1, 64:64 + TW], 1.0, None, ALU.add))
            step(V.tensor_scalar(ctrl[0:1, WSLOT, :], ctrl[0:1, WSLOT, :], 1, None, ALU.bitwise_and))

            V.scalar_tensor_tensor(edge_v[:, 0, :], src_f[:, :], 2048.0, dst_f[:, :], ALU.mult, ALU.add)
            V.scalar_tensor_tensor(edge_v[:, 1, :], hi_f[:, 0, :], float(P), lo_f[:, 0, :], ALU.mult, ALU.add)
            step(V.scalar_tensor_tensor(edge_v[:, 2, :], src_f[:, :], float(P), dp1_f[:, :], ALU.mult, ALU.add))

            def onehots(c, u):
                def col(a):
                    return a[:, bass.ds(c, 1)]

                V.tensor_scalar(oh_lo1[u][:, :], iota_f[0:EP, 0:P], col(lo_f[:, 0, :]), None, ALU.is_equal)
                V.tensor_scalar(oh_m1[u][:, :], iota_f[0:EP, 0:MSG_TILES], col(hi_f[:, 0, :]),
                                col(edge_v[:, 0, :]), ALU.is_equal, ALU.mult)
                V.tensor_scalar(oh_d[u][:, :], iota_h[0:EP, 1:P + 1], col(dp1_f[:, :]), None, ALU.is_equal)
                V.tensor_scalar(oh_c[u][:, :], iota_h[0:EP, :], col(cell_f[:, :]), None,
                                ALU.is_equal).then_inc(s_hot, 1)

            def dst_onehots(c, u):
                def col(a):
                    return a[:, bass.ds(c, 1)]

                V.tensor_scalar(oh_lo2[u][:, :], iota_f[0:EP, 0:P], col(lo_f[:, 1, :]), None, ALU.is_equal)
                for n in range(2):
                    last = V.tensor_scalar(oh_m2[u][:, n, :], iota_f[0:EP, 0:AGG_TILES], col(hi_f[:, 1, :]),
                                           col(edge_v[:, 1 + n, :]), ALU.is_equal, ALU.mult)
                last.then_inc(s_hot2, 1)

            for c in range(2):
                onehots(c, c)
            with dve.Fori(1, ET // 2) as j:
                for u in range(2):
                    dve.wait_ge(s_tab, 2 * j + (u - 1))
                    onehots(2 * j + u, u)

            for a in (idx_src, idx_cell, idx_msg, idx_xw):
                V.memset(a[:, :], 0)
            step(V.memset(dloc[:, :], -1.0))
            dve.wait_ge(s_tab, ET)
            M = MSG_TILES
            step(V.tensor_copy(word[:, 0, 0:M], psT[0][:, 0:M]))
            step(V.tensor_scalar(word[:, 1, 0:M], word[:, 0, 0:M], 2047, None, ALU.bitwise_and))
            V.tensor_scalar(idx_src[:, 0:M], word[:, 0, 0:M], 11, None, ALU.arith_shift_right)
            V.scalar_tensor_tensor(idx_cell[:, 0:M], word[:, 1, 0:M], float(R), rel_t[:, 0:M],
                                   ALU.mult, ALU.add)
            step(V.tensor_copy(cnt[:, :, :], psT[0][0:ND, BANK:BANK + NB * R].rearrange("p (b r) -> p b r", b=NB)))
            V.tensor_reduce(deg[:, 0, :], cnt[:, :, :], AX.X, ALU.add)
            step(V.tensor_scalar(inv[:, :, :], cnt[:, :, :], 1.0, None, ALU.max))
            V.tensor_scalar(deg[:, 0, :], deg[:, 0, :], 1.0, None, ALU.add).then_inc(s_deg, 1)
            V.reciprocal(inv[:, :, :], inv[:, :, :]).then_inc(s_inv, 1)
            V.memset(selector[0][0:1, 0:1], 0.0).then_inc(s_tables, 1)
            dve.wait_ge(s_sdeg, 1)
            inverse_sqrt(dinv[:, :], deg[:, 0, :], deg[:, 1, :], deg[:, 2, :])

            dve.wait_ge(s_whi, 2)
            split_lo(1).then_inc(s_wlo, 1)

            def tile_lo(t, u):
                dve.wait_ge(s_hi, t + 1)
                V.tensor_tensor(alo[u][:, :, :], tview(0, P), ahi[u][:, :, :].bitcast(f32),
                                ALU.subtract).then_inc(s_lo, 1)

            def split_next_lo(t):
                first = dve.value_load(ctrl[0:1, FIRST, bass.ds(t, 1)], min_val=0, max_val=1)
                rel = dve.value_load(ctrl[0:1, REL, bass.ds(t, 1)], min_val=0, max_val=R - 1)
                slot = dve.value_load(ctrl[0:1, WSLOT, bass.ds(t, 1)], min_val=0, max_val=1)
                with dve.If(first == 1):
                    dve.wait_ge(s_whi, rel + 3)
                    dve.sem_inc(s_passed)
                    V.tensor_tensor(
                        wr[:, bass.ds(1 - slot, 1), 1, :, :].rearrange("p o c n -> p (o c) n"), wraw[:, :, :],
                        wr[:, bass.ds(1 - slot, 1), 0, :, :].rearrange("p o c n -> p (o c) n").bitcast(f32),
                        ALU.subtract).then_inc(s_wlo, 1)

            columns = [True]

            def pair(j):
                for u in range(2):
                    tile_lo(2 * j + (u + 1), 1 - u)
                    if columns[0]:
                        if not first_pair(j):
                            dve.wait_ge(s_tab2, 2 * j + (u - 1))
                        dst_onehots(2 * j + u, u)
                    split_next_lo(2 * j + u)

            def unpack():
                columns[0] = False
                A = AGG_TILES
                dve.wait_ge(s_tab2, ET)
                V.tensor_copy(idx_msg[:, 0:A], psT[1][:, 0:A])
                step(V.tensor_copy(word[:, 0, 0:A], psT[1][:, A:2 * A]))
                V.tensor_scalar(idx_xw[:, 0:A], word[:, 0, 0:A], 7, None, ALU.arith_shift_right)
                step(V.tensor_scalar(word[:, 1, 0:A], word[:, 0, 0:A], P - 1, None, ALU.bitwise_and))
                V.tensor_scalar(dloc[:, 0:A], word[:, 1, 0:A], -1.0, None, ALU.add).then_inc(s_tables2, 1)

            tile_lo(0, 0)
            every_pair(dve, pair, unpack)

            def aggregate(ph):
                def select(w, u):
                    V.tensor_scalar(selector[u][:, :], iota_f[:, 0:P], dloc[:, bass.ds(w, 1)], None,
                                    ALU.is_equal).then_inc(s_sel[ph], 1)

                def add(w, u):
                    blk = dve.value_load(ctrl[0:1, BLK, bass.ds(w, 1)], min_val=0, max_val=NB - 1)
                    dve.wait_ge(s_ap[ph], w + 1)
                    if not (isinstance(w, int) and w == 0):
                        dve.wait_ge(s_aa[ph], w)
                    into = acc[:, bass.ds(blk, 1), :].rearrange("p o (h n) -> p (o h) n", h=2)
                    V.tensor_tensor(into, yview(u, ND), into, ALU.add).then_inc(s_aa[ph], 1)

                select(0, 0)
                for w in range(2):
                    select(w + 1, 1 - w)
                    add(w, w)
                with dve.Fori(1, AGG_TILES // 2) as j:
                    for u in range(2):
                        select(2 * j + (u + 1), 1 - u)
                        add(2 * j + u, u)
                dve.wait_ge(s_aa[ph], AGG_TILES)

            aggregate(0)
            V.memset(selector[0][0:1, 0:1], 0.0).then_inc(s_h1, 1)
            for b in range(NB):
                dense_lo(b, NB + b)
            dve.wait_ge(s_xw, NB)
            dve.wait_ge(s_xwst, 16)
            aggregate(1)
            dve.wait_ge(s_xb, NB)
            for b in range(NB):
                V.scalar_tensor_tensor(xt[:, b, :], acc[:, b, :], dinv[:, b:b + 1], xt[:, b, :],
                                       ALU.mult, ALU.add).then_inc(s_fin, 1)

        @block.tensor
        def _(pe):
            mm = nc.tensor.matmul

            def transpose_block(b, n):
                if n >= 2:
                    pe.wait_ge(s_dlo, n - 1)
                for c in range(KC):
                    last = nc.tensor.transpose(tview(b % 2, ND)[:, c, :], acc[:, b, c * P:(c + 1) * P],
                                               ident[0:ND, 0:ND])
                last.then_inc(s_dT, 1)

            def product(a, m, w_hi, w_lo, u):
                for h in range(2):
                    o = psY[u][0:m, h * BANK:h * BANK + HALF]
                    for c in range(KC):
                        hi, lo = ahi[a][:, c, 0:m], alo[a][:, c, 0:m]
                        mm(o, hi, w_hi(c, h), start=(c == 0), stop=False)
                        mm(o, hi, w_lo(c, h), start=False, stop=False)
                        last = mm(o, lo, w_hi(c, h), start=False, stop=(c == KC - 1))
                return last

            def static_w(slot, part):
                return lambda c, h: wr[:, slot, part, c, h * HALF:(h + 1) * HALF]

            def dense(slot, n0, layer, ready, freed):
                for b in range(NB + 1):
                    if b < NB:
                        ready(b)
                        transpose_block(b, n0 + b)
                    if b >= 1:
                        k = b - 1
                        pe.wait_ge(s_dlo, n0 + k + 1)
                        if k == 0:
                            pe.wait_ge(s_wlo, layer + 1)
                        freed(k)
                        product(k % 2, ND, static_w(slot, 0), static_w(slot, 1), k % 2).then_inc(s_dprod, 1)

            def h_ready(b):
                if b == 0:
                    pe.wait_ge(s_dve, 2 * NB + 7)
                pe.wait_ge(s_h, b + 1)

            def root_freed(k):
                if k >= 2:
                    pe.wait_ge(s_dev, k - 1)

            dense(0, 0, 0, h_ready, root_freed)

            pe.wait_ge(s_dev, NB)
            pe.wait_ge(s_sm_in, 1)
            mm(psY[0][0:G, 0:1], tot[:, :], ones[0:EP, 0:1], start=True, stop=True).then_inc(s_sm, 1)
            pe.wait_ge(s_sm_in, 2)
            o = psY[1][0:EP, 8:8 + G]
            mm(o, tri[0:EP, 0:EP], tot[:, :], start=True, stop=False)
            mm(o, c128[0:G, 0:EP], tri_t[:, :], start=False, stop=True).then_inc(s_sm, 1)
            mm(psY[1][0:G, BANK:BANK + 1], tri_t[:, :], ones[0:G, 0:1], start=True, stop=True).then_inc(s_sm, 1)
            pe.wait_ge(s_sm_in, 3)
            mm(psY[0][:, 64:64 + TW], masks[:, 0, :], cmpt[:, 0, :], start=True, stop=True).then_inc(s_sm, 1)
            mm(psY[0][:, BANK:BANK + TW], masks[:, 1, :], cmpt[:, 1, :], start=True, stop=True).then_inc(s_sm, 1)
            mm(psY[1][:, BANK:BANK + TW], masks[:, 2, :], cmpt[:, 0, :], start=True, stop=True).then_inc(s_sm, 1)
            mm(psY[1][:, BANK + TW:BANK + TW + 1], masks[:, 1, :], ncol[:, 2:3], start=True,
               stop=True).then_inc(s_sm, 1)

            def move(u, start, stop):
                mm(psT[0][:, 0:MSG_TILES], oh_lo1[u][:, :], oh_m1[u][:, :], start=start, stop=stop)
                mm(psT[0][:, BANK:BANK + NB * R], oh_d[u][:, :], oh_c[u][:, :], start=start,
                   stop=stop).then_inc(s_tab, 1)

            pe.wait_ge(s_hot, 1)
            move(0, True, False)
            with pe.Fori(0, ET // 2 - 1) as j:
                for u in (1, 0):
                    pe.wait_ge(s_hot, 2 * j + (2 if u else 3))
                    move(u, False, False)
            pe.wait_ge(s_hot, ET)
            move(1, False, True)

            def dst_move(c, u, start, stop):
                pe.wait_ge(s_hot2, c + 1)
                mm(psT[1][:, 0:2 * AGG_TILES], oh_lo2[u][:, :],
                   oh_m2[u][:, :, :].rearrange("p v t -> p (v t)"), start=start, stop=stop,
                   skip_group_check=True).then_inc(s_tab2, 1)

            def tile_transpose(t, u, count):
                pe.wait_ge(s_rows[u], 16 * count)
                for c in range(KC):
                    last = nc.tensor.transpose(tview(0, P)[:, c, :], rows[u][:, c * P:(c + 1) * P], ident[:, :])
                last.then_inc(s_T, 1)

            def tile_product(t, u):
                rel = pe.value_load(ctrl[0:1, REL, bass.ds(t, 1)], min_val=0, max_val=R - 1)
                slot = pe.value_load(ctrl[0:1, WSLOT, bass.ds(t, 1)], min_val=0, max_val=1)
                pe.wait_ge(s_wlo, rel + 2)
                part = [wr[:, bass.ds(slot, 1), k, :, :].rearrange("p o c n -> p (o c) n") for k in range(2)]
                product(u, P, lambda c, h: part[0][:, c, h * HALF:(h + 1) * HALF],
                        lambda c, h: part[1][:, c, h * HALF:(h + 1) * HALF], u).then_inc(s_prod, 1)

            columns = [True]

            def pair(j):
                for u in range(2):
                    pe.wait_ge(s_lo, 2 * j + (u + 1))
                    tile_transpose(2 * j + (u + 1), 1 - u, j + (1 + u))
                    if not first_pair(j):
                        pe.wait_ge(s_evac, 2 * j + (u - 1))
                    tile_product(2 * j + u, u)
                    if columns[0]:
                        dst_move(2 * j + u, u, first_pair(j) and u == 0, False)

            def columns_done():
                columns[0] = False

            pe.wait_ge(s_tables, 1)
            tile_transpose(0, 0, 1)
            every_pair(pe, pair, columns_done)
            pe.wait_ge(s_evac, tiles_done(pe))

            def aggregate(ph):
                def sums(w, u, count):
                    pe.wait_ge(s_sel[ph], w + 1)
                    pe.wait_ge(s_g6[ph][u], 16 * count)
                    for h in range(2):
                        last = mm(psY[u % 2][0:ND, h * BANK:h * BANK + HALF], selector[u % 2][:, 0:ND],
                                  rows6[:, u, :][:, h * HALF:(h + 1) * HALF], start=True, stop=True)
                    last.then_inc(s_ap[ph], 1)

                for u in range(U):
                    if u >= 2:
                        pe.wait_ge(s_aa[ph], u - 1)
                    sums(u, u, 1)
                with pe.Fori(1, AGG_TILES // U) as j:
                    for u in range(U):
                        pe.wait_ge(s_aa[ph], U * j + (u - 1))
                        sums(U * j + u, u, j + 1)

            aggregate(0)
            pe.wait_ge(s_h1, 1)

            def xw_freed(k):
                if k >= 2:
                    pe.wait_ge(s_xw, k - 1)

            dense((R + 1) % 2, NB, R + 1, lambda b: None, xw_freed)
            aggregate(1)


_INS = ['x', 'src', 'dst', 'edge_type_34', 'L0_gnn_W_rel', 'L0_gnn_W_root', 'L0_gnn_b_rgcn', 'L0_gnn_W_gcn',
        'L0_gnn_b_gcn']
_OUTS = [((1250, 768), 'float32')]


def kernel(**inputs):
    import numpy as _np
    import concourse.bacc as _bacc
    from concourse import mybir as _mybir
    from concourse.bass_utils import run_bass_kernel_spmd as _run

    nc = _bacc.Bacc("TRN2", target_bir_lowering=False, num_devices=1)
    arrays, args = {}, []
    for name in _INS:
        a = _np.ascontiguousarray(inputs[name])
        arrays[f"in_{name}_dram"] = a
        args.append(nc.dram_tensor(f"in_{name}_dram", a.shape, _mybir.dt.from_np(a.dtype), kind="ExternalInput").ap())
    for i, (shape, dtype) in enumerate(_OUTS):
        dt = _mybir.dt.from_np(_np.dtype(dtype))
        args.append(nc.dram_tensor(f"out_{i}_dram", shape, dt, kind="ExternalOutput").ap())
    relational_gnn_kernel(nc, *args)
    r = _run(nc, [arrays], core_ids=[0])
    got = tuple(r.results[0][f"out_{i}_dram"] for i in range(len(_OUTS)))
    return got[0]
```

```python
import concourse.bass as bass
from concourse import mybir
from contextlib import ExitStack


def relational_gnn_kernel(
    nc: bass.Bass,
    x: bass.AP,
    src: bass.AP,
    dst: bass.AP,
    edge_type: bass.AP,
    W_rel: bass.AP,
    W_root: bass.AP,
    b_rgcn: bass.AP,
    W_gcn: bass.AP,
    b_gcn: bass.AP,
    out: bass.AP,
):
    f32, f32r, f16, i32 = mybir.dt.float32, mybir.dt.float32r, mybir.dt.float16, mybir.dt.int32
    ALU = mybir.AluOpType
    ACT = mybir.ActivationFunctionType
    AX = mybir.AxisListType

    P = 128
    N, D = x.shape
    E = src.shape[0]
    R = W_rel.shape[0]
    ND, NB = 125, 10
    EP, ET = 125, 160
    assert ND * NB == N and EP * ET == E
    KC = D // P
    HALF = D // 2
    BANK = 512
    G = R + NB
    MSG_TILES = (E + R * P) // P
    U = 6
    AGG_TILES = -(-((E + NB * (P - 1)) // P) // U) * U
    TW = 192
    assert MSG_TILES % 2 == 0 and max(MSG_TILES, AGG_TILES) < TW
    LAYERS = R + 2
    WN = KC * D
    EPS = 1e-5
    SURE_PAIRS = ET // 2
    assert 2 * SURE_PAIRS <= MSG_TILES and ET % 2 == 0
    AGG_GROUPS = AGG_TILES // U
    SURE_GROUPS = -(-E // (U * P))
    LAYER, BLK, TOTAL = range(3)

    h_dram = nc.dram_tensor("h_rows", (N, D), f32, kind="Internal").ap()
    msg_dram = nc.dram_tensor("message_rows", (MSG_TILES * P, D), f32, kind="Internal").ap()
    inv_dram = nc.dram_tensor("inverse_counts", (N * R, 1), f32, kind="Internal").ap()
    xw_dram = nc.dram_tensor("xw_rows", (N, D), f32, kind="Internal").ap()

    def nodes(ap):
        return ap.rearrange("(b d) f -> d b f", b=NB)

    def weights(ap):
        return ap.rearrange("(c p) n -> p c n", c=KC)

    with ExitStack() as ctx:
        def sb(name, shape, dt):
            return ctx.enter_context(nc.sbuf_tensor(name, shape, dt))

        def sem(name):
            return ctx.enter_context(nc.semaphore(name))

        ring_at = -(-nc.sbuf_base // 32) * 32
        sb("ring_memory", [P, 5 * WN], f32)
        free_at = [ring_at + 8 * WN]

        def placed(name, shape, dt, size):
            here = free_at[0]
            free_at[0] += -(-size // 32) * 32
            assert free_at[0] <= ring_at + 16 * WN
            return nc.alloc_sbuf_tensor_at(name, shape, dt, offset=here)

        wr = nc.alloc_sbuf_tensor_at("w_ring", [P, 2, 2, KC, D], f32r, offset=ring_at)
        wraw = nc.alloc_sbuf_tensor_at("w_raw", [P, KC, D], f32, offset=ring_at + 16 * WN)
        rows6 = wraw
        xt = sb("x_nodes", [ND, NB, D], f32)
        acc = sb("acc", [ND, NB, D], f32)
        rows = [sb(f"h_gathered{u}", [P, D], f32) for u in range(2)]
        ahi = [sb(f"a_hi{u}", [P, KC, P], f32r) for u in range(2)]
        alo = [sb(f"a_lo{u}", [P, KC, P], f32r) for u in range(2)]
        ysb = [sb(f"y_out{u}", [P, D], f32) for u in range(2)]
        idx_src = sb("idx_src", [P, TW], i32)
        idx_cell = sb("idx_cell", [P, TW], i32)
        idx_msg = sb("idx_msg", [P, TW], i32)
        idx_xw = sb("idx_xw", [P, TW], i32)
        dloc = sb("dst_local", [P, TW], f32)
        ctrl = sb("ctrl", [1, 3, TW], i32)
        dinv = sb("dinv", [ND, NB], f32)
        degree = sb("degree_kept", [ND, NB], f32)
        ident = sb("identity", [P, P], f32)
        iota_i = sb("iota_i", [P, R * NB], i32)
        iota_f = sb("iota_f", [P, TW], f32)
        iota_h = sb("iota_h", [P, R * NB], f16)
        part_i = sb("part_i", [P, 1], i32)
        part_f = sb("part_f", [P, 1], f32)
        idxbuf = [sb(f"idxbuf{u}", [P, 1], i32) for u in range(U)]
        cellbuf = [sb(f"cellbuf{u}", [P, 1], i32) for u in range(2)]
        invbuf = [sb(f"invbuf{u}", [P, 1], f32) for u in range(2)]
        selector = [sb(f"selector{u}", [P, P], f32) for u in range(3)]

        psT = [ctx.enter_context(nc.psum_tensor(f"psT{u}", [P, 2 * BANK], f32)) for u in range(2)]
        psY = [ctx.enter_context(nc.psum_tensor(f"psY{u}", [P, 2 * BANK], f32)) for u in range(2)]

        def tview(u, m):
            return psT[u][:, 0:D].rearrange("p (c m) -> p c m", c=KC)[:, :, 0:m]

        def yview(u, m):
            return psY[u][0:m, :].rearrange("p (h n) -> p h n", h=2)[:, :, 0:HALF]

        def agg_psum(n):
            bank = (psY[0], psY[1], psT[0])[n]
            return bank[0:ND, :].rearrange("p (h n) -> p h n", h=2)[:, :, 0:HALF]

        def halves(ap):
            return ap.rearrange("p (h n) -> p h n", h=2)

        s_edges, s_x, s_bias = sem("edges_loaded"), sem("x_loaded"), sem("bias_loaded")
        s_iota = sem("iota_made")
        s_dve = sem("vector_step")
        s_zero, s_fill = sem("zero_rows_made"), sem("zero_rows_stored")
        s_stats, s_std, s_norm = sem("stats_ready"), sem("std_ready"), sem("norm_ready")
        s_h, s_hst = sem("h_ready"), sem("h_stored")
        s_ctrl = sem("control_table_ready")
        s_dp1, s_dist, s_hotd = sem("dst_numbers_ready"), sem("distances_ready"), sem("dst_in_block_onehots_ready")
        s_wload, s_whi, s_wlo = sem("w_loaded"), sem("w_hi_ready"), sem("w_lo_ready")
        s_dT, s_dhi, s_dlo = sem("dense_transposed"), sem("dense_hi"), sem("dense_lo")
        s_dprod, s_dev = sem("dense_product"), sem("dense_evacuated")
        s_sm_in, s_sm = sem("small_operand"), sem("small_product")
        s_hot, s_tab = sem("onehots_ready"), sem("onehots_used")
        s_hot2, s_tab2 = sem("dst_onehots_ready"), sem("dst_onehots_used")
        s_tables2 = sem("dst_tables_ready")
        s_inv, s_invst = sem("inverse_ready"), sem("inverse_stored")
        s_deg, s_sdeg = sem("degree_ready"), sem("sqrt_degree_ready")
        s_tables = sem("tables_ready")
        s_rowi, s_celli = sem("row_index_copied"), sem("cell_index_copied")
        s_xb = sem("x_plus_bias")
        s_rows = [sem(f"rows_gathered{u}") for u in range(2)]
        s_invg = [sem(f"inverse_gathered{u}") for u in range(2)]
        s_T, s_hi, s_lo = sem("tile_transposed"), sem("tile_hi"), sem("tile_lo")
        s_prod, s_evac = sem("tile_product"), sem("tile_evacuated")
        s_yst = [sem(f"messages_stored{u}") for u in range(2)]
        s_g6 = [[sem(f"agg{ph}_gathered{u}") for u in range(U)] for ph in range(2)]
        s_ai = [sem(f"agg{ph}_index") for ph in range(2)]
        s_sel = [sem(f"agg{ph}_selector") for ph in range(2)]
        s_ap = [sem(f"agg{ph}_product") for ph in range(2)]
        s_aa = [sem(f"agg{ph}_added") for ph in range(2)]
        s_h1 = sem("h1_complete")
        s_passed = sem("waits_passed")
        s_xw, s_xwst = sem("xw_ready"), sem("xw_stored")
        s_fin, s_fin2, s_out = sem("even_out_ready"), sem("odd_out_ready"), sem("out_stored")
        s_self = sem("start_sums_ready")

        prep = ctx.enter_context(ExitStack())

        def tmp(name, shape, dt):
            return prep.enter_context(nc.sbuf_tensor(name, shape, dt))

        edges_i = placed("edges_i", [EP, 3, ET], i32, 12 * ET)
        src_f, dst_f, rel_f, blk_f, dp1_f, cell_f = (
            placed(name, [EP, ET], f32, 4 * ET) for name in ("src_f", "dst_f", "rel_f", "blk_f", "dp1_f", "cell_f"))
        scan_at = free_at[0]
        scan = placed("group_scan", [EP, G * ET], mybir.dt.int16, 2 * G * ET)
        pos_f = placed("pos_f", [EP, 2, ET], f32, 8 * ET)
        pos_i = placed("pos_i", [EP, 2, ET], i32, 8 * ET)
        DEEP = 8
        distance = rows[1][0:EP, :].bitcast(f16)[:, 0:DEEP * P].rearrange("p (k n) -> p k n", k=DEEP)
        hot_at = free_at[0]
        hot = placed("group_onehot", [EP, G, ET], mybir.dt.int16, 2 * G * ET)
        lo_i = pos_f[:, :, :].bitcast(i32)
        lo_f = tmp("lo_f", [EP, 2, ET], f32)
        hi_f = tmp("hi_f", [EP, 2, ET], f32)
        edge_v = tmp("edge_values", [EP, 3, ET], f32)
        tot = tmp("totals", [EP, G], f32)
        tots = tmp("totals_scan", [EP, G], f32)
        delta = tmp("delta", [EP, G], f32)
        savec = tmp("first_column", [EP, G], f32)
        tri = tmp("tri", [P, P], f32)
        ones = tmp("ones", [P, P], f32)
        c128 = tmp("c128", [P, P], f32)
        mcol = tmp("mask_columns", [P, 8], f32)
        masks = tmp("masks", [G, 3, P], f32)
        ncol = tmp("group_sizes", [G, 4], f32)
        ncol_i = tmp("group_sizes_i", [G, 2], i32)
        tri_t = tmp("tri_tiles", [G, G], f32)
        cmpt = tmp("starts_compared", [G, 2, TW], f32)
        rel_t = tmp("rel_of_tile", [P, TW], f32)
        stats = tmp("bn_stats", [ND, 2, 6], f32)
        mv = tmp("mean_var", [ND, NB, 2], f32)
        nrm = tmp("norm", [ND, 3, NB], f32)
        brow, bgcn = ysb[0][0:ND, :], ysb[1][0:ND, :]
        free_at[0] = scan_at
        oh_d = placed("dst_onehots", [EP, 2, DEEP, P], f16, 4 * DEEP * P)
        free_at[0] = hot_at
        oh_lo1 = [placed(f"oh_lo1{u}", [EP, P], f16, 2 * P) for u in range(DEEP)]
        oh_m1 = [placed(f"oh_m1{u}", [EP, 2, MSG_TILES], f16, 4 * MSG_TILES) for u in range(DEEP)]
        oh_c = [placed(f"oh_c{u}", [EP, NB * R], f16, 2 * NB * R) for u in range(DEEP)]
        oh_lo2 = [tmp(f"oh_lo2{u}", [EP, P], f16) for u in range(2)]
        oh_m2 = [tmp(f"oh_m2{u}", [EP, 3, AGG_TILES], f16) for u in range(2)]
        word = tmp("table_words", [P, 5, TW], i32)
        cnt = tmp("cell_counts", [ND, NB, R], f32)
        inv = tmp("inverse", [ND, NB, R], f32)
        deg = tmp("degree", [ND, 3, NB], f32)

        block = ctx.enter_context(nc.Block())

        def static_view(t):
            return t[:, :, :].rearrange("p c n -> p (c n)")

        def first_pair(j):
            return isinstance(j, int) and j == 0

        def every_pair(eng, pair, between=None):
            pair(0)
            with eng.Fori(1, SURE_PAIRS) as j:
                pair(j)
            if between:
                between()
            total = tiles_done(eng)
            with eng.Fori(SURE_PAIRS, MSG_TILES // 2) as j:
                with eng.If(2 * j < total):
                    pair(j)

        def layer_of(eng, t):
            word = eng.value_load(ctrl[0:1, LAYER, bass.ds(t, 1)], min_val=0, max_val=4 * R - 1)
            return word // 4, (word // 2) % 2, word % 2

        def tiles_done(eng):
            return eng.value_load(ctrl[0:1, TOTAL, 0:1], min_val=2 * SURE_PAIRS, max_val=MSG_TILES)

        def later_groups(eng, group):
            with eng.Fori(1, SURE_GROUPS) as j:
                group(j)
            total = dst_tiles_done(eng)
            with eng.Fori(SURE_GROUPS, AGG_GROUPS) as j:
                with eng.If(U * j < total):
                    group(j)

        def dst_tiles_done(eng):
            return eng.value_load(ctrl[0:1, TOTAL, 1:2], min_val=U * SURE_GROUPS, max_val=AGG_TILES)

        @block.sync
        def _(sp):
            for n, a in enumerate((src, dst, edge_type)):
                sp.dma_start(edges_i[:, n, :], a.rearrange("(p t) -> p t", p=EP)).then_inc(s_edges, 16)
            sp.dma_start(xt[:, :, :], nodes(x)).then_inc(s_x, 16)
            sp.dma_start(wraw[:, :, :], weights(W_root)).then_inc(s_wload, 16)
            sp.dma_start(brow, b_rgcn.partition_broadcast(ND)).then_inc(s_bias, 16)
            sp.dma_start(bgcn, b_gcn.partition_broadcast(ND)).then_inc(s_bias, 16)
            spare = (MSG_TILES - 2 * SURE_PAIRS) * P * D // (P * P)
            sp.wait_ge(s_zero, 1)
            sp.dma_start(msg_dram[2 * SURE_PAIRS * P:, :].rearrange("r (k d) -> (r k) d", d=P)
                         .rearrange("(n p) d -> p n d", p=P),
                         selector[0][:, :].unsqueeze(1).broadcast_to((P, spare, P))).then_inc(s_fill, 16)
            with sp.Fori(0, R) as r:
                sp.wait_ge(s_wlo, 2 * r + 2)
                sp.wait_ge(s_whi, 2 * r + 2)
                sp.dma_start(wraw[:, :, :],
                             W_rel[bass.ds(r, 1), :, :].rearrange("o (c p) n -> p (o c) n", c=KC)
                             ).then_inc(s_wload, 16)
            sp.wait_ge(s_wlo, 2 * R + 2)
            sp.wait_ge(s_whi, 2 * R + 2)
            sp.dma_start(wraw[:, :, :], weights(W_gcn)).then_inc(s_wload, 16)
            for b in range(NB):
                sp.wait_ge(s_xw, b + 1)
                sp.dma_start(xw_dram[b * ND:(b + 1) * ND, :], acc[:, b, :]).then_inc(s_xwst, 16)
            for b in range(0, NB, 2):
                for n, ready in enumerate((s_fin, s_fin2)):
                    sp.wait_ge(ready, b // 2 + 1)
                    sp.dma_start(out[(b + n) * ND:(b + n + 1) * ND, :], acc[:, b + n, :]).then_inc(s_out, 16)
            sp.wait_ge(s_out, 16 * NB)

        @block.gpsimd
        def _(pool):
            nc.gpsimd.iota(iota_i[:, :], [[1, R * NB]], base=0, channel_multiplier=0).then_inc(s_iota, 1)
            nc.gpsimd.iota(part_i[:, :], [[0, 1]], base=0, channel_multiplier=1).then_inc(s_iota, 1)

            nc.gpsimd.memset(selector[0][:, :], 0.0).then_inc(s_zero, 1)

            for n in range(2):
                cs = slice(n * KC // 2, (n + 1) * KC // 2)
                pool.wait_ge(s_whi, n + 1)
                nc.gpsimd.tensor_tensor(wr[:, 0, 1, cs, :], wraw[:, cs, :], wr[:, 0, 0, cs, :].bitcast(f32),
                                        ALU.subtract).then_inc(s_wlo, 1)

            pool.wait_ge(s_bias, 32)
            for b in range(NB):
                pool.wait_ge(s_h, b + 1)
                nc.gpsimd.tensor_tensor(xt[:, b, :], xt[:, b, :], bgcn, ALU.add).then_inc(s_xb, 1)

            pool.wait_ge(s_tables, 1)
            pool.wait_ge(s_hst, 16 * NB)

            def gather_h(t, u):
                nc.gpsimd.tensor_copy(idxbuf[u][:, :], idx_src[:, bass.ds(t, 1)]).then_inc(s_rowi, 1)
                pool.wait_ge(s_rowi, t + 1)
                pool.sem_inc(s_passed)
                nc.gpsimd.indirect_dma_start(
                    rows[u][:, :], None, h_dram,
                    bass.IndirectOffsetOnAxis(idxbuf[u][:, 0:1], 0)).then_inc(s_rows[u], 16)

            def gather_inverse(t, u):
                nc.gpsimd.tensor_copy(cellbuf[u][:, :], idx_cell[:, bass.ds(t, 1)]).then_inc(s_celli, 1)
                pool.wait_ge(s_celli, t + 1)
                pool.sem_inc(s_passed)
                nc.gpsimd.indirect_dma_start(
                    invbuf[u][:, :], None, inv_dram,
                    bass.IndirectOffsetOnAxis(cellbuf[u][:, 0:1], 0)).then_inc(s_invg[u], 16)

            def pair(j):
                for u in range(2):
                    pool.wait_ge(s_T, 2 * j + (u + 1))
                    gather_h(2 * j + (u + 2), u)
                    if not first_pair(j):
                        pool.wait_ge(s_evac, 2 * j + (u - 1))
                        pool.sem_inc(s_passed)
                    gather_inverse(2 * j + u, u)

            for u in range(2):
                gather_h(u, u)
            pool.wait_ge(s_invst, 16)
            pool.wait_ge(s_fill, 16)
            every_pair(pool, pair)

            def gather_rows(ph, w, u, index, table):
                nc.gpsimd.tensor_copy(idxbuf[u][:, :], index[:, bass.ds(w, 1)]).then_inc(s_ai[ph], 1)
                pool.wait_ge(s_ai[ph], w + 1)
                pool.sem_inc(s_passed)
                nc.gpsimd.indirect_dma_start(
                    rows6[:, u, :], None, table,
                    bass.IndirectOffsetOnAxis(idxbuf[u][:, 0:1], 0)).then_inc(s_g6[ph][u], 16)

            for ph, index, table in ((0, idx_msg, msg_dram), (1, idx_xw, xw_dram)):
                if ph == 0:
                    pool.wait_ge(s_tables2, 1)
                    for u in range(2):
                        pool.wait_ge(s_yst[u], tiles_done(pool) * 8)
                        pool.sem_inc(s_passed)
                    pool.wait_ge(s_whi, 2 * LAYERS)
                    pool.wait_ge(s_wlo, 2 * LAYERS)
                else:
                    pool.wait_ge(s_xwst, 16 * NB)
                for u in range(U):
                    gather_rows(ph, u, u, index, table)

                def group(j):
                    for u in range(U):
                        pool.wait_ge(s_ap[ph], U * j + (u - U + 1))
                        gather_rows(ph, U * j + u, u, index, table)

                later_groups(pool, group)

        @block.scalar
        def _(act):
            def split_hi(dest):
                for n in range(2):
                    cs = slice(n * KC // 2, (n + 1) * KC // 2)
                    nc.scalar.copy(dest(cs), wraw[:, cs, :]).then_inc(s_whi, 1)

            def distances(g):
                if not (isinstance(g, int) and g == 0):
                    act.wait_ge(s_hotd, g)
                for k in range(DEEP):
                    last = nc.scalar.activation(distance[:, k, :], iota_h[0:EP, 1:P + 1], ACT.Abs,
                                                bias=dp1_f[:, bass.ds(g * DEEP + k, 1)], scale=-1.0)
                last.then_inc(s_dist, 1)

            def in_block_onehots(g, half):
                act.wait_ge(s_dist, g + 1)
                nc.scalar.activation(oh_d[:, half, :, :], distance[:, :, :], ACT.Relu,
                                     bias=ones[0:EP, 0:1], scale=-1.0).then_inc(s_hotd, 1)

            act.wait_ge(s_dp1, 1)
            distances(0)
            act.wait_ge(s_wload, 16)
            split_hi(lambda cs: wr[:, 0, 0, cs, :])
            act.wait_ge(s_stats, 1)
            nc.scalar.activation(nrm[:, 0, :], nrm[:, 1, :], ACT.Sqrt).then_inc(s_std, 1)
            act.wait_ge(s_norm, 1)
            act.wait_ge(s_x, 16)

            def dense_hi(n):
                act.wait_ge(s_dT, n + 1)
                nc.scalar.copy(ahi[0][:, :, 0:ND], tview(0, ND)).then_inc(s_dhi, 1)

            def root_block(b):
                if not first_pair(b):
                    act.wait_ge(s_tab, b * (ET // NB) - DEEP)
                    distances(2 * b)
                    in_block_onehots(2 * b, 0)
                    act.wait_ge(s_dT, b)
                    act.wait_ge(s_hst, 16 * b)
                nc.scalar.activation(rows[0][0:ND, :].unsqueeze(1), xt[:, bass.ds(b, 1), :], ACT.Relu,
                                     bias=nrm[:, 2, bass.ds(b, 1)],
                                     scale=nrm[:, 1, bass.ds(b, 1)]).then_inc(s_h, 1)
                act.wait_ge(s_h, b + 1)
                act.dma_start(h_dram[bass.ds(b * ND, ND), :], rows[0][0:ND, :]).then_inc(s_hst, 16)
                if first_pair(b):
                    act.wait_ge(s_ctrl, 1)
                    in_block_onehots(0, 0)
                else:
                    act.wait_ge(s_tab, b * (ET // NB))
                distances(2 * b + 1)
                in_block_onehots(2 * b + 1, 1)
                if not first_pair(b):
                    act.wait_ge(s_dprod, b)
                dense_hi(b)

            root_block(0)
            with act.Fori(1, NB) as b:
                root_block(b)
            act.wait_ge(s_wload, 32)
            act.wait_ge(s_tab, ET)
            split_hi(lambda cs: wr[:, 1, 0, cs, :])
            act.wait_ge(s_inv, 1)
            act.dma_start(inv_dram.rearrange("(b d r) o -> d b (r o)", b=NB, r=R),
                          inv[:, :, :]).then_inc(s_invst, 16)
            act.wait_ge(s_deg, 1)
            nc.scalar.activation(deg[:, 1, :], deg[:, 0, :], ACT.Sqrt).then_inc(s_sdeg, 1)
            act.wait_ge(s_ctrl, 1)

            def tile_hi(t, u):
                act.wait_ge(s_T, t + 1)
                nc.scalar.copy(ahi[u][:, :, :], tview(0, P)).then_inc(s_hi, 1)

            def split_next_hi(t, very_first):
                rel, slot, first = layer_of(act, t)
                with act.If(first == 1):
                    if not very_first:
                        act.wait_ge(s_prod, t)
                    act.wait_ge(s_wload, rel * 16 + 48)
                    split_hi(lambda cs: wr[:, bass.ds(1 - slot, 1), 0, cs, :].rearrange("p o c n -> p (o c) n"))

            def tile_out(t, u, j):
                act.wait_ge(s_prod, t + 1)
                act.wait_ge(s_invg[u], 16 * j + 16)
                if not first_pair(j):
                    act.wait_ge(s_yst[u], 16 * j)
                nc.scalar.activation(halves(ysb[u][:, :]), yview(u, P), ACT.Copy,
                                     scale=invbuf[u][:, 0:1]).then_inc(s_evac, 1)
                act.wait_ge(s_evac, t + 1)
                act.dma_start(msg_dram[bass.ds(t * P, P), :], ysb[u][:, :]).then_inc(s_yst[u], 16)

            def pair(j):
                for u in range(2):
                    if not (first_pair(j) and u == 0):
                        act.wait_ge(s_prod, 2 * j + u)
                    tile_hi(2 * j + (u + 1), 1 - u)
                    split_next_hi(2 * j + u, first_pair(j) and u == 0)
                    tile_out(2 * j + u, u, j)

            tile_hi(0, 0)
            every_pair(act, pair)

            def gcn_out(b):
                act.wait_ge(s_dprod, NB + b + 1)
                nc.scalar.activation(halves(acc[:, b, :]), yview(b % 2, ND), ACT.Copy,
                                     scale=dinv[:, b:b + 1]).then_inc(s_xw, 1)

            for b in range(NB):
                act.wait_ge(s_dT, NB + b + 1)
                if b >= 2:
                    act.wait_ge(s_dprod, NB + b - 1)
                nc.scalar.copy(ahi[b % 2][:, :, 0:ND], tview(0, ND)).then_inc(s_dhi, 1)
                if b:
                    gcn_out(b - 1)
            gcn_out(NB - 1)
            act.wait_ge(s_aa[1], dst_tiles_done(act))
            act.sem_inc(s_passed)
            act.wait_ge(s_xwst, 16 * NB)
            for b in range(1, NB, 2):
                nc.scalar.mul(acc[:, b, :], xt[:, b, :], dinv[:, b:b + 1]).then_inc(s_fin2, 1)

        @block.vector
        def _(dve):
            chain = [0]
            V = nc.vector

            def step(ins):
                chain[0] += 1
                ins.then_inc(s_dve, 1)
                dve.wait_ge(s_dve, chain[0])

            def inverse_sqrt(y, v, root, t):
                step(V.reciprocal(root, root))
                step(V.tensor_tensor(t, root, root, ALU.mult))
                step(V.scalar_tensor_tensor(t, t, -0.5, v, ALU.mult, ALU.mult))
                step(V.tensor_scalar(t, t, 1.5, None, ALU.add))
                step(V.tensor_tensor(y, root, t, ALU.mult))

            dve.wait_ge(s_iota, 2)
            V.tensor_copy(part_f[:, :], part_i[:, :])
            V.tensor_copy(iota_h[:, :], iota_i[:, :])
            V.memset(ones[:, :], 1.0)
            V.memset(c128[:, :], float(P))
            step(V.tensor_copy(iota_f[:, :], iota_i[:, 0:TW]))
            V.tensor_scalar(tri[:, :], iota_f[:, 0:P], part_f[:, 0:1], None, ALU.is_gt)
            V.tensor_scalar(mcol[:, 0:1], part_f[:, :], 1.0, None, ALU.is_ge)
            V.tensor_scalar(mcol[:, 1:2], part_f[:, :], float(R), None, ALU.is_lt)
            V.tensor_scalar(mcol[:, 2:3], part_f[:, :], float(R + 1), None, ALU.is_ge)
            V.tensor_scalar(mcol[:, 5:6], part_f[:, :], float(R), None, ALU.is_ge)
            step(V.tensor_scalar(ident[:, :], iota_f[:, 0:P], part_f[:, 0:1], None, ALU.is_equal))
            V.tensor_scalar(masks[:, 0, :], ones[0:G, :], mcol[0:G, 0:1], mcol[0:G, 1:2], ALU.mult, ALU.mult)
            V.tensor_scalar(masks[:, 1, :], ones[0:G, :], mcol[0:G, 1:2], None, ALU.mult)
            step(V.tensor_scalar(masks[:, 2, :], ones[0:G, :], mcol[0:G, 2:3], None, ALU.mult))

            def split_lo(dest, layer2):
                for n in range(2):
                    cs = slice(n * KC // 2, (n + 1) * KC // 2)
                    dve.wait_ge(s_whi, layer2 + (n + 1))
                    if not isinstance(layer2, int):
                        dve.sem_inc(s_passed)
                    V.tensor_tensor(dest(1, cs), wraw[:, cs, :], dest(0, cs).bitcast(f32),
                                    ALU.subtract).then_inc(s_wlo, 1)

            def edges_to_float():
                dve.wait_ge(s_edges, 48)
                V.tensor_copy(src_f[:, :], edges_i[:, 0, :])
                V.tensor_copy(dst_f[:, :], edges_i[:, 1, :])
                step(V.tensor_copy(rel_f[:, :], edges_i[:, 2, :]))

            def node_block():
                step(V.tensor_scalar(blk_f[:, :], dst_f[:, :], float(ND), None, ALU.is_ge))
                for k in range(2, NB):
                    step(V.scalar_tensor_tensor(blk_f[:, :], dst_f[:, :], float(k * ND), blk_f[:, :],
                                                ALU.is_ge, ALU.add))
                step(V.scalar_tensor_tensor(dp1_f[:, :], blk_f[:, :], -float(ND), dst_f[:, :],
                                            ALU.mult, ALU.add))
                V.scalar_tensor_tensor(cell_f[:, :], blk_f[:, :], float(R), rel_f[:, :], ALU.mult, ALU.add)
                step(V.tensor_scalar(dp1_f[:, :], dp1_f[:, :], 1.0, None, ALU.add))
                V.tensor_copy(edge_v[:, 2, :], src_f[:, :]).then_inc(s_dp1, 1)

            def relation_onehot():
                step(V.tensor_tensor(hot[:, 0:R, :], rel_f[:, :].unsqueeze(1).broadcast_to((EP, R, ET)),
                                     iota_f[0:EP, 0:R].unsqueeze(2).broadcast_to((EP, R, ET)), ALU.is_equal))

            def block_onehot():
                step(V.tensor_tensor(hot[:, R:G, :], blk_f[:, :].unsqueeze(1).broadcast_to((EP, NB, ET)),
                                     iota_f[0:EP, 0:NB].unsqueeze(2).broadcast_to((EP, NB, ET)), ALU.is_equal))

            def totals():
                step(V.tensor_reduce(tot[:, :], hot[:, :, :], AX.X, ALU.add))
                step(V.tensor_tensor_scan(tots[:, :], tot[:, :], tot[:, :], 0.0, ALU.add, ALU.max))

            edges_to_float()
            node_block()
            relation_onehot()
            block_onehot()
            totals()
            V.tensor_copy(tri_t[:, :], tri[0:G, 0:G]).then_inc(s_sm_in, 1)

            dve.wait_ge(s_x, 16)
            for b in range(NB):
                V.bn_stats(stats[:, 0, :], xt[:, b, 0:HALF])
                step(V.bn_stats(stats[:, 1, :], xt[:, b, HALF:D]))
                step(V.bn_aggr(mv[:, b, :], stats[:, :, :].rearrange("p a b -> p (a b)")))
            V.tensor_scalar(nrm[:, 1, :], mv[:, :, 1], EPS, None, ALU.add).then_inc(s_stats, 1)
            dve.wait_ge(s_std, 1)
            inverse_sqrt(nrm[:, 1, :], nrm[:, 1, :], nrm[:, 0, :], nrm[:, 2, :])
            V.scalar_tensor_tensor(nrm[:, 2, :], mv[:, :, 0], -1.0, nrm[:, 1, :],
                                   ALU.mult, ALU.mult).then_inc(s_norm, 1)

            dve.wait_ge(s_sm, 1)
            step(V.tensor_scalar(ncol[:, 0:1], psY[0][0:G, 0:1], float(P - 1), None, ALU.add))
            step(V.tensor_copy(ncol_i[:, 0:1], ncol[:, 0:1]))
            step(V.tensor_scalar(ncol_i[:, 1:2], ncol_i[:, 0:1], 7, None, ALU.arith_shift_right))
            step(V.tensor_copy(ncol[:, 1:2], ncol_i[:, 1:2]))
            step(V.tensor_scalar(ncol[:, 2:3], ncol[:, 1:2], mcol[0:G, 1:2], None, ALU.max))
            step(V.tensor_scalar(tri_t[:, 0:R], tri_t[:, 0:R], ncol[:, 2:3], None, ALU.mult))
            step(V.tensor_scalar(tri_t[:, R:G], tri_t[:, R:G], ncol[:, 2:3], masks[:, 2, 0:1],
                                 ALU.mult, ALU.mult))
            step(V.tensor_scalar(mcol[0:G, 3:4], part_f[0:G, :], float(R), None, ALU.is_equal))
            step(V.tensor_scalar(mcol[0:G, 4:5], ncol[:, 2:3], mcol[0:G, 3:4], None, ALU.mult))
            V.scalar_tensor_tensor(tri_t[:, R:G], tri[0:G, R:G], mcol[0:G, 4:5], tri_t[:, R:G],
                                   ALU.mult, ALU.add).then_inc(s_sm_in, 1)
            dve.wait_ge(s_sm, 2)
            step(V.tensor_tensor(delta[:, :], psY[1][0:EP, 8:8 + G], tots[:, :], ALU.subtract))
            step(V.tensor_tensor(delta[:, :], delta[:, :], tot[:, :], ALU.add))
            step(V.tensor_copy(savec[:, :], hot[:, :, 0]))
            V.tensor_tensor(hot[:, 0:1, 0], savec[:, 0:1], delta[:, 0:1], ALU.add)
            step(V.tensor_tensor(hot[:, 1:G, 0], savec[:, 1:G], delta[:, 1:G], ALU.add))
            step(V.tensor_tensor(hot[:, 1:G, 0], hot[:, 1:G, 0], delta[:, 0:G - 1], ALU.subtract))
            hot2 = hot[:, :, :].rearrange("p g t -> p (g t)")
            step(V.tensor_tensor_scan(scan[:, :], hot2, hot2, 0.0, ALU.add, ALU.bypass))
            step(V.tensor_copy(hot[:, :, 0], savec[:, :]))
            step(V.tensor_tensor(scan[:, :], scan[:, :], hot2, ALU.mult))
            scan3 = scan[:, :].rearrange("p (g t) -> p t g", g=G)
            V.tensor_reduce(pos_f[:, 0, :], scan3[:, :, 0:R], AX.X, ALU.add)
            step(V.tensor_reduce(pos_f[:, 1, :], scan3[:, :, R:G], AX.X, ALU.add))
            step(V.tensor_scalar(pos_i[:, :, :], pos_f[:, :, :], -1.0, None, ALU.add))
            step(V.tensor_scalar(lo_i, pos_i[:, :, :], P - 1, None, ALU.bitwise_and))
            step(V.tensor_scalar(pos_i[:, :, :], pos_i[:, :, :], 7, None, ALU.arith_shift_right))
            V.tensor_copy(lo_f[:, :, :], lo_i)
            step(V.tensor_copy(hi_f[:, :, :], pos_i[:, :, :]))
            step(V.tensor_scalar(pos_i[:, 1, :], lo_i[:, 0, :], 15, None, ALU.bitwise_and))
            step(V.tensor_copy(pos_f[:, 1, :], pos_i[:, 1, :]))
            step(V.scalar_tensor_tensor(edge_v[:, 1, :], pos_f[:, 1, :], float(P), dp1_f[:, :],
                                        ALU.mult, ALU.add))
            step(V.tensor_tensor(pos_f[:, 0, :], lo_f[:, 0, :], pos_f[:, 1, :], ALU.subtract))
            step(V.tensor_scalar(pos_f[:, 0, :], pos_f[:, 0, :], 1.0 / 16, None, ALU.mult))
            step(V.scalar_tensor_tensor(edge_v[:, 0, :], hi_f[:, 0, :], 8.0, pos_f[:, 0, :],
                                        ALU.mult, ALU.add))
            dve.wait_ge(s_sm, 3)
            step(V.tensor_copy(ncol[:, 3:4], psY[1][0:G, BANK:BANK + 1]))
            V.tensor_scalar(cmpt[:, 0, :], iota_f[0:G, :], ncol[:, 3:4], None, ALU.is_ge)
            V.tensor_scalar(cmpt[:, 1, :], iota_f[0:G, :], ncol[:, 3:4], None,
                            ALU.is_equal).then_inc(s_sm_in, 1)
            dve.wait_ge(s_sm, 8)
            V.tensor_copy(ctrl[0:1, BLK, :], psY[1][0:1, BANK:BANK + TW])
            step(V.tensor_copy(rel_t[:, :], psY[0][:, 64:64 + TW]))
            step(V.tensor_scalar(word[0:1, 0, :], rel_t[0:1, :], 1.0, None, ALU.add))
            step(V.tensor_scalar(word[0:1, 1, :], word[0:1, 0, :], 1, 1, ALU.bitwise_and, ALU.logical_shift_left))
            step(V.tensor_tensor(word[0:1, 2, :], psY[0][0:1, BANK:BANK + TW], word[0:1, 1, :], ALU.add))
            V.scalar_tensor_tensor(ctrl[0:1, LAYER, :], rel_t[0:1, :], 4.0, word[0:1, 2, :],
                                   ALU.mult, ALU.add)
            step(V.tensor_scalar(ctrl[0:1, TOTAL, 0:1], psY[1][0:1, BANK + TW:BANK + TW + 1], 1.0,
                                 float(2 * SURE_PAIRS), ALU.add, ALU.max))
            step(V.tensor_scalar(ctrl[0:1, TOTAL, 0:1], ctrl[0:1, TOTAL, 0:1], 1, 1,
                                 ALU.arith_shift_right, ALU.logical_shift_left))
            V.tensor_scalar(tots[0:1, 0:AGG_GROUPS], iota_f[0:1, 0:AGG_GROUPS], float(U), None, ALU.mult)
            step(V.tensor_copy(savec[0:1, 0:1], psY[1][0:1, BANK + TW + 1:BANK + TW + 2]))
            step(V.tensor_scalar(tots[0:1, 0:AGG_GROUPS], tots[0:1, 0:AGG_GROUPS], savec[0:1, 0:1], None,
                                 ALU.is_lt))
            step(V.tensor_reduce(savec[0:1, 1:2], tots[0:1, 0:AGG_GROUPS], AX.X, ALU.add))
            V.tensor_scalar(ctrl[0:1, TOTAL, 1:2], savec[0:1, 1:2], float(U), float(U * SURE_GROUPS),
                            ALU.mult, ALU.max).then_inc(s_ctrl, 1)

            def onehots(c, u):
                def col(a):
                    return a[:, bass.ds(c, 1)]

                V.tensor_scalar(oh_lo1[u][:, :], iota_h[0:EP, 0:P], col(lo_f[:, 0, :]), None, ALU.is_equal)
                for n, value in enumerate((src_f, dst_f)):
                    V.tensor_scalar(oh_m1[u][:, n, :], iota_h[0:EP, 0:MSG_TILES], col(hi_f[:, 0, :]),
                                    col(value[:, :]), ALU.is_equal, ALU.mult)
                V.tensor_scalar(oh_c[u][:, :], iota_h[0:EP, :], col(cell_f[:, :]), None,
                                ALU.is_equal).then_inc(s_hot, 1)

            def dst_onehots(c, u):
                def col(a):
                    return a[:, bass.ds(c, 1)]

                V.tensor_scalar(oh_lo2[u][:, :], iota_h[0:EP, 0:P], col(lo_f[:, 1, :]), None, ALU.is_equal)
                for n in range(3):
                    last = V.tensor_scalar(oh_m2[u][:, n, :], iota_h[0:EP, 0:AGG_TILES], col(hi_f[:, 1, :]),
                                           col(edge_v[:, n, :]), ALU.is_equal, ALU.mult)
                last.then_inc(s_hot2, 1)

            def root_block(b):
                for i in range(ET // NB):
                    c = b * (ET // NB) + i
                    if not (first_pair(b) and i < DEEP):
                        dve.wait_ge(s_tab, b * (ET // NB) + (i - DEEP + 1))
                    onehots(c, i % DEEP)
                    if i == 5:
                        dve.wait_ge(s_dhi, b + 1)
                        V.tensor_tensor(alo[0][:, :, 0:ND], tview(0, ND), ahi[0][:, :, 0:ND].bitcast(f32),
                                        ALU.subtract).then_inc(s_dlo, 1)
                dve.wait_ge(s_dprod, b + 1)
                V.tensor_tensor(acc[:, bass.ds(b, 1), :].rearrange("p o (h n) -> p (o h) n", h=2),
                                yview(0, ND), halves(brow), ALU.add).then_inc(s_dev, 1)

            dve.wait_ge(s_bias, 32)
            root_block(0)
            with dve.Fori(1, NB) as b:
                root_block(b)

            for a in (idx_src, idx_cell, idx_msg, idx_xw):
                V.memset(a[:, :], 0)
            step(V.memset(dloc[:, :], -1.0))
            dve.wait_ge(s_tab, ET)
            M = MSG_TILES
            V.tensor_copy(idx_src[:, 0:M], psT[1][:, 0:M])
            V.scalar_tensor_tensor(idx_cell[:, 0:M], psT[1][:, M:2 * M], float(R), rel_t[:, 0:M],
                                   ALU.mult, ALU.add).then_inc(s_tables, 1)
            step(V.tensor_copy(cnt[:, :, :], psT[1][0:ND, BANK:BANK + NB * R].rearrange("p (b r) -> p b r", b=NB)))
            V.tensor_reduce(deg[:, 0, :], cnt[:, :, :], AX.X, ALU.add)
            step(V.tensor_scalar(inv[:, :, :], cnt[:, :, :], 1.0, None, ALU.max))
            V.tensor_scalar(deg[:, 0, :], deg[:, 0, :], 1.0, None, ALU.add).then_inc(s_deg, 1)
            V.reciprocal(inv[:, :, :], inv[:, :, :]).then_inc(s_inv, 1)

            split_lo(lambda part, cs: wr[:, 1, part, cs, :], 2)

            def tile_lo(t, u):
                dve.wait_ge(s_hi, t + 1)
                V.tensor_tensor(alo[u][:, :, :], tview(0, P), ahi[u][:, :, :].bitcast(f32),
                                ALU.subtract).then_inc(s_lo, 1)

            def split_next_lo(t):
                rel, slot, first = layer_of(dve, t)
                with dve.If(first == 1):
                    split_lo(lambda part, cs: wr[:, bass.ds(1 - slot, 1), part, cs, :]
                             .rearrange("p o c n -> p (o c) n"), 2 * rel + 4)

            columns = [True]

            def pair(j):
                for u in range(2):
                    tile_lo(2 * j + (u + 1), 1 - u)
                    if columns[0]:
                        if not first_pair(j):
                            dve.wait_ge(s_tab2, 2 * j + (u - 1))
                        dst_onehots(2 * j + u, u)
                    split_next_lo(2 * j + u)

            def unpack():
                columns[0] = False
                A = AGG_TILES
                dve.wait_ge(s_tab2, ET)
                V.tensor_copy(idx_xw[:, 0:A], psT[1][:, 2 * A:3 * A])
                V.tensor_copy(word[:, 0, 0:A], psT[1][:, 0:A])
                step(V.tensor_copy(word[:, 1, 0:A], psT[1][:, A:2 * A]))
                step(V.tensor_scalar(word[:, 2, 0:A], word[:, 1, 0:A], 7, None, ALU.arith_shift_right))
                V.scalar_tensor_tensor(idx_msg[:, 0:A], word[:, 0, 0:A], 16.0, word[:, 2, 0:A],
                                       ALU.mult, ALU.add)
                step(V.tensor_scalar(word[:, 3, 0:A], word[:, 1, 0:A], P - 1, None, ALU.bitwise_and))
                V.tensor_scalar(dloc[:, 0:A], word[:, 3, 0:A], -1.0, None, ALU.add).then_inc(s_tables2, 1)
                dve.wait_ge(s_sdeg, 1)
                V.tensor_copy(degree[:, :], deg[:, 0, :])
                inverse_sqrt(dinv[:, :], deg[:, 0, :], deg[:, 1, :], deg[:, 2, :])

            tile_lo(0, 0)
            every_pair(dve, pair, unpack)

            def aggregate(ph, into):
                def select(w, u):
                    V.tensor_scalar(selector[u][:, :], iota_f[:, 0:P], dloc[:, bass.ds(w, 1)], None,
                                    ALU.is_equal).then_inc(s_sel[ph], 1)

                def add(w, u):
                    blk = dve.value_load(ctrl[0:1, BLK, bass.ds(w, 1)], min_val=0, max_val=NB - 1)
                    dve.wait_ge(s_ap[ph], w + 1)
                    if not (isinstance(w, int) and w == 0):
                        dve.wait_ge(s_aa[ph], w)
                    sums = into[:, bass.ds(blk, 1), :].rearrange("p o (h n) -> p (o h) n", h=2)
                    V.tensor_tensor(sums, agg_psum(u), sums, ALU.add).then_inc(s_aa[ph], 1)

                select(0, 0)
                select(1, 1)
                for w in range(U):
                    select(w + 2, (w + 2) % 3)
                    add(w, w % 3)

                def group(j):
                    for u in range(U):
                        select(U * j + (u + 2), (u + 2) % 3)
                        add(U * j + u, u % 3)

                later_groups(dve, group)
                dve.wait_ge(s_aa[ph], dst_tiles_done(dve))
                dve.sem_inc(s_passed)

            dve.wait_ge(s_fill, 16)
            aggregate(0, acc)
            V.memset(word[0:1, 0, 0:1], 0).then_inc(s_h1, 1)
            step(V.tensor_tensor(deg[:, 1, :], degree[:, :], dinv[:, :], ALU.mult))

            def sums_start(b):
                dve.wait_ge(s_xw, b + 1)
                V.scalar_tensor_tensor(xt[:, b, :], xt[:, b, :], deg[:, 1, b:b + 1], acc[:, b, :],
                                       ALU.mult, ALU.add).then_inc(s_self, 1)

            dve.wait_ge(s_xb, NB)
            for b in range(NB):
                dve.wait_ge(s_dhi, NB + b + 1)
                V.tensor_tensor(alo[b % 2][:, :, 0:ND], tview(0, ND), ahi[b % 2][:, :, 0:ND].bitcast(f32),
                                ALU.subtract).then_inc(s_dlo, 1)
                if b >= 2:
                    sums_start(b - 2)
            sums_start(NB - 2)
            sums_start(NB - 1)
            dve.wait_ge(s_self, NB)
            aggregate(1, xt)
            dve.wait_ge(s_xwst, 16 * NB)
            for b in range(0, NB, 2):
                V.tensor_scalar(acc[:, b, :], xt[:, b, :], dinv[:, b:b + 1], None, ALU.mult).then_inc(s_fin, 1)

        @block.tensor
        def _(pe):
            mm = nc.tensor.matmul

            def transpose_block(source, n):
                for c in range(KC):
                    last = nc.tensor.transpose(tview(0, ND)[:, c, :], source[:, c * P:(c + 1) * P],
                                               ident[0:ND, 0:ND])
                last.then_inc(s_dT, 1)

            def product(a, m, w_hi, w_lo, u, hs=(0, 1)):
                for h in hs:
                    o = psY[u][0:m, h * BANK:h * BANK + HALF]
                    for c in range(KC):
                        hi, lo = ahi[a][:, c, 0:m], alo[a][:, c, 0:m]
                        mm(o, hi, w_hi(c, h), start=(c == 0), stop=False)
                        mm(o, hi, w_lo(c, h), start=False, stop=False)
                        last = mm(o, lo, w_hi(c, h), start=False, stop=(c == KC - 1))
                return last

            def static_w(slot, part):
                return lambda c, h: wr[:, slot, part, c, h * HALF:(h + 1) * HALF]

            pe.wait_ge(s_sm_in, 1)
            mm(psY[0][0:G, 0:1], tot[:, :], ones[0:EP, 0:1], start=True, stop=True).then_inc(s_sm, 1)
            pe.wait_ge(s_sm_in, 2)
            o = psY[1][0:EP, 8:8 + G]
            mm(o, tri[0:EP, 0:EP], tot[:, :], start=True, stop=False)
            mm(o, c128[0:G, 0:EP], tri_t[:, :], start=False, stop=True).then_inc(s_sm, 1)
            mm(psY[1][0:G, BANK:BANK + 1], tri_t[:, :], ones[0:G, 0:1], start=True, stop=True).then_inc(s_sm, 1)
            pe.wait_ge(s_sm_in, 3)
            mm(psY[0][:, 64:64 + TW], masks[:, 0, :], cmpt[:, 0, :], start=True, stop=True).then_inc(s_sm, 1)
            mm(psY[0][:, BANK:BANK + TW], masks[:, 1, :], cmpt[:, 1, :], start=True, stop=True).then_inc(s_sm, 1)
            mm(psY[1][:, BANK:BANK + TW], masks[:, 2, :], cmpt[:, 0, :], start=True, stop=True).then_inc(s_sm, 1)
            mm(psY[1][:, BANK + TW:BANK + TW + 1], masks[:, 1, :], ncol[:, 2:3], start=True,
               stop=True).then_inc(s_sm, 1)
            mm(psY[1][0:1, BANK + TW + 1:BANK + TW + 2], mcol[0:G, 5:6], ncol[:, 2:3], start=True,
               stop=True).then_inc(s_sm, 1)

            def move(b, i, start):
                pe.wait_ge(s_hot, b * (ET // NB) + (i + 1))
                u = i % DEEP
                if i % DEEP == 0:
                    pe.wait_ge(s_hotd, 2 * b + (i // DEEP + 1))
                mm(psT[1][:, 0:2 * MSG_TILES], oh_lo1[u][:, :], oh_m1[u][:, :, :].rearrange("p v t -> p (v t)"),
                   start=start, stop=False, skip_group_check=True)
                mm(psT[1][:, BANK:BANK + NB * R], oh_d[:, i // DEEP, u, :], oh_c[u][:, :], start=start, stop=False,
                   skip_group_check=True).then_inc(s_tab, 1)

            def root_block(b):
                for i in range(ET // NB):
                    move(b, i, first_pair(b) and i == 0)
                    if i == 2:
                        pe.wait_ge(s_h, b + 1)
                        if not first_pair(b):
                            pe.wait_ge(s_dlo, b)
                        transpose_block(rows[0][0:ND, :], b)
                    if i == 6:
                        pe.wait_ge(s_dlo, b + 1)
                        if first_pair(b):
                            pe.wait_ge(s_wlo, 2)
                            pe.wait_ge(s_ctrl, 1)
                        else:
                            pe.wait_ge(s_dev, b)
                        product(0, ND, static_w(0, 0), static_w(0, 1), 0, (0,))
                    if i == 10:
                        product(0, ND, static_w(0, 0), static_w(0, 1), 0, (1,)).then_inc(s_dprod, 1)

            root_block(0)
            with pe.Fori(1, NB) as b:
                root_block(b)

            def dst_move(c, u, start, stop):
                pe.wait_ge(s_hot2, c + 1)
                mm(psT[1][:, 0:3 * AGG_TILES], oh_lo2[u][:, :],
                   oh_m2[u][:, :, :].rearrange("p v t -> p (v t)"), start=start, stop=stop,
                   skip_group_check=True).then_inc(s_tab2, 1)

            def tile_transpose(t, u, count):
                pe.wait_ge(s_rows[u], 16 * count)
                for c in range(KC):
                    last = nc.tensor.transpose(tview(0, P)[:, c, :], rows[u][:, c * P:(c + 1) * P], ident[:, :])
                last.then_inc(s_T, 1)

            def tile_product(t, u):
                rel, slot, _ = layer_of(pe, t)
                pe.wait_ge(s_wlo, 2 * rel + 4)
                part = [wr[:, bass.ds(slot, 1), k, :, :].rearrange("p o c n -> p (o c) n") for k in range(2)]
                product(u, P, lambda c, h: part[0][:, c, h * HALF:(h + 1) * HALF],
                        lambda c, h: part[1][:, c, h * HALF:(h + 1) * HALF], u).then_inc(s_prod, 1)

            columns = [True]

            def pair(j):
                for u in range(2):
                    pe.wait_ge(s_lo, 2 * j + (u + 1))
                    tile_transpose(2 * j + (u + 1), 1 - u, j + (1 + u))
                    if not first_pair(j):
                        pe.wait_ge(s_evac, 2 * j + (u - 1))
                    tile_product(2 * j + u, u)
                    if columns[0]:
                        dst_move(2 * j + u, u, first_pair(j) and u == 0, False)

            def columns_done():
                columns[0] = False

            pe.wait_ge(s_tables, 1)
            tile_transpose(0, 0, 1)
            every_pair(pe, pair, columns_done)
            pe.wait_ge(s_evac, tiles_done(pe))

            def aggregate(ph):
                def sums(w, u, count):
                    pe.wait_ge(s_sel[ph], w + 1)
                    pe.wait_ge(s_g6[ph][u], 16 * count)
                    for h in range(2):
                        last = mm(agg_psum(u % 3)[:, h, :], selector[u % 3][:, 0:ND],
                                  rows6[:, u, :][:, h * HALF:(h + 1) * HALF], start=True, stop=True)
                    last.then_inc(s_ap[ph], 1)

                for u in range(U):
                    if u >= 3:
                        pe.wait_ge(s_aa[ph], u - 2)
                    sums(u, u, 1)

                def group(j):
                    for u in range(U):
                        pe.wait_ge(s_aa[ph], U * j + (u - 2))
                        sums(U * j + u, u, j + 1)

                later_groups(pe, group)

            aggregate(0)

            slot = (R + 1) % 2
            pe.wait_ge(s_h1, 1)
            transpose_block(acc[:, 0, :], NB)
            for b in range(NB):
                pe.wait_ge(s_dlo, NB + b + 1)
                if b < NB - 1:
                    transpose_block(acc[:, b + 1, :], NB + b + 1)
                if b >= 2:
                    pe.wait_ge(s_xw, b - 1)
                product(b % 2, ND, static_w(slot, 0), static_w(slot, 1), b % 2).then_inc(s_dprod, 1)
            pe.wait_ge(s_xw, NB)
            aggregate(1)


_INS = ['x', 'src', 'dst', 'edge_type_34', 'L0_gnn_W_rel', 'L0_gnn_W_root', 'L0_gnn_b_rgcn', 'L0_gnn_W_gcn',
        'L0_gnn_b_gcn']
_OUTS = [((1250, 768), 'float32')]


def kernel(**inputs):
    import numpy as _np
    import concourse.bacc as _bacc
    from concourse import mybir as _mybir
    from concourse.bass_utils import run_bass_kernel_spmd as _run

    nc = _bacc.Bacc("TRN2", target_bir_lowering=False, num_devices=1)
    arrays, args = {}, []
    for name in _INS:
        a = _np.ascontiguousarray(inputs[name])
        arrays[f"in_{name}_dram"] = a
        args.append(nc.dram_tensor(f"in_{name}_dram", a.shape, _mybir.dt.from_np(a.dtype), kind="ExternalInput").ap())
    for i, (shape, dtype) in enumerate(_OUTS):
        dt = _mybir.dt.from_np(_np.dtype(dtype))
        args.append(nc.dram_tensor(f"out_{i}_dram", shape, dt, kind="ExternalOutput").ap())
    relational_gnn_kernel(nc, *args)
    r = _run(nc, [arrays], core_ids=[0])
    got = tuple(r.results[0][f"out_{i}_dram"] for i in range(len(_OUTS)))
    return got[0]
```

```python
import concourse.bass as bass
from concourse import mybir
from contextlib import ExitStack


def relational_gnn_kernel(
    nc: bass.Bass,
    x: bass.AP,
    src: bass.AP,
    dst: bass.AP,
    edge_type: bass.AP,
    W_rel: bass.AP,
    W_root: bass.AP,
    b_rgcn: bass.AP,
    W_gcn: bass.AP,
    b_gcn: bass.AP,
    out: bass.AP,
):
    f32, f32r, f16, i32 = mybir.dt.float32, mybir.dt.float32r, mybir.dt.float16, mybir.dt.int32
    ALU = mybir.AluOpType
    ACT = mybir.ActivationFunctionType
    AX = mybir.AxisListType

    P = 128
    N, D = x.shape
    E = src.shape[0]
    R = W_rel.shape[0]
    ND, NB = 125, 10
    EP, ET = 125, 160
    assert ND * NB == N and EP * ET == E
    RECIPROCAL = (1 << 20) // ND + 1
    assert N * RECIPROCAL < 1 << 24 and all(n * RECIPROCAL >> 20 == n // ND for n in range(N))
    KC = D // P
    HALF = D // 2
    BANK = 512
    G = R + NB
    MSG_TILES = (E + R * P) // P
    U = 6
    AGG_TILES = -(-((E + NB * (P - 1)) // P) // U) * U
    TW = 192
    assert MSG_TILES % 2 == 0 and max(MSG_TILES, AGG_TILES) < TW
    assert MSG_TILES * P + ET < 1 << 15
    LAYERS = R + 2
    WN = KC * D
    EPS = 1e-5
    EARLY = 2
    COLS = ET // (NB - EARLY)
    assert COLS * (NB - EARLY) == ET
    SURE_PAIRS = ET // 2
    assert 2 * SURE_PAIRS <= MSG_TILES and ET % 2 == 0 and (MSG_TILES - 2 * SURE_PAIRS) % NB == 0
    AGG_GROUPS = AGG_TILES // U
    SURE_GROUPS = -(-E // (U * P))
    LAYER, BLK, TOTAL, END = range(4)

    h_dram = nc.dram_tensor("h_rows", (N, D), f32, kind="Internal").ap()
    msg_dram = nc.dram_tensor("message_rows", (MSG_TILES * P, D), f32, kind="Internal").ap()
    inv_dram = nc.dram_tensor("inverse_counts", (N * R, 1), f32, kind="Internal").ap()
    xw_dram = nc.dram_tensor("xw_rows", (N, D), f32, kind="Internal").ap()

    def nodes(ap):
        return ap.rearrange("(b d) f -> d b f", b=NB)

    def weights(ap):
        return ap.rearrange("(c p) n -> p c n", c=KC)

    with ExitStack() as ctx:
        def sb(name, shape, dt):
            return ctx.enter_context(nc.sbuf_tensor(name, shape, dt))

        def sem(name):
            return ctx.enter_context(nc.semaphore(name))

        ring_at = -(-nc.sbuf_base // 32) * 32
        sb("ring_memory", [P, 5 * WN], f32)
        free_at = [ring_at + 8 * WN]

        def placed(name, shape, dt, size):
            here = free_at[0]
            free_at[0] += -(-size // 32) * 32
            assert free_at[0] <= ring_at + 16 * WN
            return nc.alloc_sbuf_tensor_at(name, shape, dt, offset=here)

        wr = nc.alloc_sbuf_tensor_at("w_ring", [P, 2, 2, KC, D], f32r, offset=ring_at)
        wraw = nc.alloc_sbuf_tensor_at("w_raw", [P, KC, D], f32, offset=ring_at + 16 * WN)
        rows6 = wraw
        xt = sb("x_nodes", [ND, NB, D], f32)
        acc = sb("acc", [ND, NB, D], f32)
        rows = [sb(f"h_gathered{u}", [P, D], f32) for u in range(2)]
        ahi = [sb(f"a_hi{u}", [P, KC, P], f32r) for u in range(2)]
        alo = [sb(f"a_lo{u}", [P, KC, P], f32r) for u in range(2)]
        ysb = [sb(f"y_out{u}", [P, D], f32) for u in range(2)]
        idx_src = sb("idx_src", [P, TW], i32)
        idx_cell = sb("idx_cell", [P, TW], i32)
        idx_msg = sb("idx_msg", [P, TW], i32)
        idx_xw = sb("idx_xw", [P, TW], i32)
        dloc = sb("dst_local", [P, TW], f32)
        ctrl = sb("ctrl", [1, 4, TW], i32)
        dinv = sb("dinv", [ND, NB], f32)
        degree = sb("degree_kept", [ND, NB], f32)
        ident = sb("identity", [P, P], f32)
        iota_i = sb("iota_i", [P, R * NB], i32)
        iota_f = sb("iota_f", [P, TW], f32)
        iota_h = sb("iota_h", [P, R * NB], f16)
        part_i = sb("part_i", [P, 1], i32)
        part_f = sb("part_f", [P, 1], f32)
        idxbuf = [sb(f"idxbuf{u}", [P, 1], i32) for u in range(U)]
        cellbuf = [sb(f"cellbuf{u}", [P, 1], i32) for u in range(2)]
        invbuf = [sb(f"invbuf{u}", [P, 1], f32) for u in range(2)]
        selector = [sb(f"selector{u}", [P, P], f32) for u in range(3)]

        psT = [ctx.enter_context(nc.psum_tensor(f"psT{u}", [P, 2 * BANK], f32)) for u in range(2)]
        psY = [ctx.enter_context(nc.psum_tensor(f"psY{u}", [P, 2 * BANK], f32)) for u in range(2)]

        def tview(u, m):
            return psT[u][:, 0:D].rearrange("p (c m) -> p c m", c=KC)[:, :, 0:m]

        def product_view(bank, m):
            return bank[0:m, :].rearrange("p (h n) -> p h n", h=2)[:, :, 0:HALF]

        def yview(u, m):
            return product_view(psY[u], m)

        def agg_psum(n):
            bank = (psY[0], psY[1], psT[0])[n]
            return bank[0:ND, :].rearrange("p (h n) -> p h n", h=2)[:, :, 0:HALF]

        def halves(ap):
            return ap.rearrange("p (h n) -> p h n", h=2)

        s_edges, s_x, s_bias = sem("edges_loaded"), sem("x_loaded"), sem("bias_loaded")
        s_iota = sem("iota_made")
        s_dve = sem("vector_step")
        s_zero, s_fill = sem("zero_rows_made"), sem("zero_rows_stored")
        s_stats, s_std, s_norm = sem("stats_ready"), sem("std_ready"), sem("norm_ready")
        s_h, s_hst = sem("h_ready"), sem("h_stored")
        s_pos, s_sums, s_ctrl = sem("places_ready"), sem("small_products_copied"), sem("control_table_ready")
        s_dp1, s_dist, s_hotd = sem("dst_numbers_ready"), sem("distances_ready"), sem("dst_in_block_onehots_ready")
        s_wload, s_whi, s_wlo = sem("w_loaded"), sem("w_hi_ready"), sem("w_lo_ready")
        s_dT, s_dhi, s_dlo = sem("dense_transposed"), sem("dense_hi"), sem("dense_lo")
        s_dprod, s_dev = sem("dense_product"), sem("dense_evacuated")
        s_sm_in, s_sm = sem("small_operand"), sem("small_product")
        s_hot, s_tab = sem("onehots_ready"), sem("onehots_used")
        s_hot2, s_tab2 = sem("dst_onehots_ready"), sem("dst_onehots_used")
        s_tables2 = sem("dst_tables_ready")
        s_inv, s_invst = sem("inverse_ready"), sem("inverse_stored")
        s_deg, s_sdeg = sem("degree_ready"), sem("sqrt_degree_ready")
        s_tables = sem("tables_ready")
        s_rowi, s_celli = sem("row_index_copied"), sem("cell_index_copied")
        s_xb, s_rb = sem("x_plus_bias"), sem("root_plus_bias")
        s_rows = [sem(f"rows_gathered{u}") for u in range(2)]
        s_invg = [sem(f"inverse_gathered{u}") for u in range(2)]
        s_T, s_hi, s_lo = sem("tile_transposed"), sem("tile_hi"), sem("tile_lo")
        s_prod, s_evac = sem("tile_product"), sem("tile_evacuated")
        s_yst = [sem(f"messages_stored{u}") for u in range(2)]
        s_g6 = [[sem(f"agg{ph}_gathered{u}") for u in range(U)] for ph in range(2)]
        s_ai = [sem(f"agg{ph}_index") for ph in range(2)]
        s_sel = [sem(f"agg{ph}_selector") for ph in range(2)]
        s_ap = [sem(f"agg{ph}_product") for ph in range(2)]
        s_aa = [sem(f"agg{ph}_added") for ph in range(2)]
        s_passed = sem("waits_passed")
        s_xw, s_xwst = sem("xw_ready"), sem("xw_stored")
        s_fin, s_out = sem("out_ready"), sem("out_stored")
        s_self = sem("start_sums_ready")

        prep = ctx.enter_context(ExitStack())

        def tmp(name, shape, dt):
            return prep.enter_context(nc.sbuf_tensor(name, shape, dt))

        edges_i = placed("edges_i", [EP, 3, ET], i32, 12 * ET)
        src_f, dst_f, rel_f, blk_f, dp1_f, cell_f = (
            placed(name, [EP, ET], f32, 4 * ET) for name in ("src_f", "dst_f", "rel_f", "blk_f", "dp1_f", "cell_f"))
        scan_at = free_at[0]
        scan = placed("group_scan", [EP, G * ET], mybir.dt.int16, 2 * G * ET)
        hot = placed("group_onehot", [EP, G, ET], mybir.dt.int16, 2 * G * ET)
        pos_at = free_at[0]
        pos_f = placed("pos_f", [EP, 2, ET], f32, 8 * ET)
        pos_i = placed("pos_i", [EP, 2, ET], i32, 8 * ET)
        DEEP = COLS // 2
        distance = rows[1][0:EP, :].bitcast(f16)[:, 0:DEEP * P].rearrange("p (k n) -> p k n", k=DEEP)
        lo_i = pos_f[:, :, :].bitcast(i32)
        lo_f = tmp("lo_f", [EP, 2, ET], f32)
        hi_f = tmp("hi_f", [EP, 2, ET], f32)
        edge_v = tmp("edge_values", [EP, 3, ET], f32)
        tot = tmp("totals", [EP, G], f32)
        tots = tmp("totals_scan", [EP, G], f32)
        delta = tmp("delta", [EP, G], f32)
        savec = tmp("first_column", [EP, G], f32)
        tri = tmp("tri", [P, P], f32)
        ones = tmp("ones", [P, P], f32)
        c128 = tmp("c128", [P, P], f32)
        mcol = tmp("mask_columns", [P, 8], f32)
        masks = tmp("masks", [G, 3, P], f32)
        ncol = tmp("group_sizes", [G, 4], f32)
        ncol_i = tmp("group_sizes_i", [G, 2], i32)
        sums = tmp("small_products", [1, 2, TW + 2 + NB], f32)
        upto = tmp("blocks_up_to", [G, NB], f32)
        tri_t = tmp("tri_tiles", [G, G], f32)
        cmpt = tmp("starts_compared", [G, 2, TW], f32)
        rel_t = tmp("rel_of_tile", [P, TW], f32)
        stats = tmp("bn_stats", [ND, 2, 6], f32)
        mv = tmp("mean_var", [ND, NB, 2], f32)
        nrm = tmp("norm", [ND, 3, NB], f32)
        brow, bgcn = ysb[0][0:ND, :], ysb[1][0:ND, :]
        free_at[0] = scan_at
        oh_d = placed("dst_onehots", [EP, 2, DEEP, P], f16, 4 * DEEP * P)
        oh_lo1 = [placed(f"oh_lo1{u}", [EP, P], f32, 4 * P) for u in range(DEEP)]
        oh_m1 = [placed(f"oh_m1{u}", [EP, MSG_TILES], f32, 4 * MSG_TILES) for u in range(DEEP)]
        oh_c = [placed(f"oh_c{u}", [EP, NB * R], f16, 2 * NB * R) for u in range(DEEP)]
        assert free_at[0] <= pos_at
        oh_lo2 = [tmp(f"oh_lo2{u}", [EP, P], f16) for u in range(2)]
        oh_m2 = [tmp(f"oh_m2{u}", [EP, 3, AGG_TILES], f16) for u in range(2)]
        word = tmp("table_words", [P, 5, TW], i32)
        cnt = tmp("cell_counts", [ND, NB, R], f32)
        inv = tmp("inverse", [ND, NB, R], f32)
        deg = tmp("degree", [ND, 3, NB], f32)

        block = ctx.enter_context(nc.Block())

        def first_pair(j):
            return isinstance(j, int) and j == 0

        def every_pair(eng, pair, between=None):
            pair(0)
            with eng.Fori(1, SURE_PAIRS) as j:
                pair(j)
            if between:
                between()
            total = tiles_done(eng)
            with eng.Fori(SURE_PAIRS, MSG_TILES // 2) as j:
                with eng.If(2 * j < total):
                    pair(j)

        def layer_of(eng, t):
            word = eng.value_load(ctrl[0:1, LAYER, bass.ds(t, 1)], min_val=0, max_val=4 * R - 1)
            return word // 4, (word // 2) % 2, word % 2

        def tiles_done(eng):
            return eng.value_load(ctrl[0:1, TOTAL, 0:1], min_val=2 * SURE_PAIRS, max_val=MSG_TILES)

        def later_groups(eng, group):
            with eng.Fori(1, SURE_GROUPS) as j:
                group(j)
            total = dst_tiles_done(eng)
            with eng.Fori(SURE_GROUPS, AGG_GROUPS) as j:
                with eng.If(U * j < total):
                    group(j)

        def dst_tiles_done(eng):
            return eng.value_load(ctrl[0:1, TOTAL, 1:2], min_val=U * SURE_GROUPS, max_val=AGG_TILES)

        def tiles_to_end(eng, b):
            if b == NB - 1:
                return dst_tiles_done(eng)
            return eng.value_load(ctrl[0:1, END, b:b + 1], min_val=1, max_val=AGG_TILES)

        @block.sync
        def _(sp):
            for n, a in enumerate((src, dst, edge_type)):
                sp.dma_start(edges_i[:, n, :], a.rearrange("(p t) -> p t", p=EP)).then_inc(s_edges, 16)
            sp.dma_start(xt[:, :, :], nodes(x)).then_inc(s_x, 16)
            sp.dma_start(wraw[:, :, :], weights(W_root)).then_inc(s_wload, 16)
            sp.dma_start(brow, b_rgcn.partition_broadcast(ND)).then_inc(s_bias, 16)
            sp.dma_start(bgcn, b_gcn.partition_broadcast(ND)).then_inc(s_bias, 16)

            def load_relation(r):
                sp.wait_ge(s_wlo, 2 * r + 2)
                sp.wait_ge(s_whi, 2 * r + 2)
                sp.dma_start(wraw[:, :, :],
                             W_rel[bass.ds(r, 1), :, :].rearrange("o (c p) n -> p (o c) n", c=KC)
                             ).then_inc(s_wload, 16)

            sp.wait_ge(s_hst, 16 * EARLY)
            load_relation(0)
            sp.wait_ge(s_zero, 1)
            part = (MSG_TILES - 2 * SURE_PAIRS) // NB * P
            spare = part * D // (P * P)
            for b in range(NB):
                sp.wait_ge(s_hst, 16 * (b + 1))
                at = 2 * SURE_PAIRS * P + b * part
                sp.dma_start(msg_dram[at:at + part, :].rearrange("r (k d) -> (r k) d", d=P)
                             .rearrange("(n p) d -> p n d", p=P),
                             selector[0][:, :].unsqueeze(1).broadcast_to((P, spare, P))).then_inc(s_fill, 16)
            with sp.Fori(1, R) as r:
                load_relation(r)
            sp.wait_ge(s_wlo, 2 * R + 2)
            sp.wait_ge(s_whi, 2 * R + 2)
            sp.dma_start(wraw[:, :, :], weights(W_gcn)).then_inc(s_wload, 16)
            for b in range(NB):
                sp.wait_ge(s_xw, b + 1)
                sp.dma_start(xw_dram[b * ND:(b + 1) * ND, :], acc[:, b, :]).then_inc(s_xwst, 16)
            for b in range(NB):
                sp.wait_ge(s_fin, b + 1)
                sp.dma_start(out[b * ND:(b + 1) * ND, :], acc[:, b, :]).then_inc(s_out, 16)
            sp.wait_ge(s_out, 16 * NB)

        @block.gpsimd
        def _(pool):
            nc.gpsimd.iota(iota_i[:, :], [[1, R * NB]], base=0, channel_multiplier=0).then_inc(s_iota, 1)
            nc.gpsimd.iota(part_i[:, :], [[0, 1]], base=0, channel_multiplier=1).then_inc(s_iota, 1)

            nc.gpsimd.memset(selector[0][:, :], 0.0).then_inc(s_zero, 1)

            for n in range(2):
                cs = slice(n * KC // 2, (n + 1) * KC // 2)
                pool.wait_ge(s_whi, n + 1)
                nc.gpsimd.tensor_tensor(wr[:, 0, 1, cs, :], wraw[:, cs, :], wr[:, 0, 0, cs, :].bitcast(f32),
                                        ALU.subtract).then_inc(s_wlo, 1)

            pool.wait_ge(s_bias, 32)
            for b in range(NB):
                pool.wait_ge(s_h, b + 1)
                nc.gpsimd.tensor_tensor(xt[:, b, :], xt[:, b, :], bgcn, ALU.add).then_inc(s_xb, 1)
                pool.wait_ge(s_dev, b + 1)
                nc.gpsimd.tensor_tensor(acc[:, b, :], acc[:, b, :], brow, ALU.add).then_inc(s_rb, 1)

            pool.wait_ge(s_tables, 1)
            pool.wait_ge(s_hst, 16 * NB)

            def gather_h(t, u):
                nc.gpsimd.tensor_copy(idxbuf[u][:, :], idx_src[:, bass.ds(t, 1)]).then_inc(s_rowi, 1)
                pool.wait_ge(s_rowi, t + 1)
                pool.sem_inc(s_passed)
                nc.gpsimd.indirect_dma_start(
                    rows[u][:, :], None, h_dram,
                    bass.IndirectOffsetOnAxis(idxbuf[u][:, 0:1], 0)).then_inc(s_rows[u], 16)

            def gather_inverse(t, u):
                nc.gpsimd.tensor_copy(cellbuf[u][:, :], idx_cell[:, bass.ds(t, 1)]).then_inc(s_celli, 1)
                pool.wait_ge(s_celli, t + 1)
                pool.sem_inc(s_passed)
                nc.gpsimd.indirect_dma_start(
                    invbuf[u][:, :], None, inv_dram,
                    bass.IndirectOffsetOnAxis(cellbuf[u][:, 0:1], 0)).then_inc(s_invg[u], 16)

            def pair(j):
                for u in range(2):
                    pool.wait_ge(s_T, 2 * j + (u + 1))
                    gather_h(2 * j + (u + 2), u)
                    if not first_pair(j):
                        pool.wait_ge(s_evac, 2 * j + (u - 1))
                        pool.sem_inc(s_passed)
                    gather_inverse(2 * j + u, u)

            for u in range(2):
                gather_h(u, u)
            pool.wait_ge(s_invst, 16)
            pool.wait_ge(s_fill, 16 * NB)
            every_pair(pool, pair)

            for ph, index, table in ((0, idx_msg, msg_dram), (1, idx_xw, xw_dram)):
                def copy_index(w, u):
                    nc.gpsimd.tensor_copy(idxbuf[u][:, :], index[:, bass.ds(w, 1)]).then_inc(s_ai[ph], 1)

                def gather_rows(w, u):
                    pool.wait_ge(s_ai[ph], w + 1)
                    pool.sem_inc(s_passed)
                    nc.gpsimd.indirect_dma_start(
                        rows6[:, u, :], None, table,
                        bass.IndirectOffsetOnAxis(idxbuf[u][:, 0:1], 0)).then_inc(s_g6[ph][u], 16)

                if ph == 0:
                    pool.wait_ge(s_tables2, 1)
                    for u in range(2):
                        pool.wait_ge(s_rows[u], tiles_done(pool) * 8 + 16)
                        pool.sem_inc(s_passed)
                else:
                    pool.wait_ge(s_ai[0], dst_tiles_done(pool) + 2)
                    pool.sem_inc(s_passed)
                copy_index(0, 0)
                copy_index(1, 1)
                if ph == 0:
                    for u in range(2):
                        pool.wait_ge(s_yst[u], tiles_done(pool) * 8)
                        pool.sem_inc(s_passed)
                    pool.wait_ge(s_whi, 2 * LAYERS)
                    pool.wait_ge(s_wlo, 2 * LAYERS)
                else:
                    pool.wait_ge(s_xwst, 16 * NB)
                for u in range(U):
                    gather_rows(u, u)
                    if u + 2 < U:
                        copy_index(u + 2, u + 2)

                def copy_ahead(j, u):
                    ahead = (u + 2) % U
                    pool.wait_ge(s_g6[ph][ahead], 16 * (j + (u + 2) // U))
                    pool.sem_inc(s_passed)
                    copy_index(U * j + (u + 2), ahead)

                copy_ahead(0, U - 2)
                copy_ahead(0, U - 1)

                def group(j):
                    for u in range(U):
                        pool.wait_ge(s_ap[ph], U * j + (u - U + 1))
                        gather_rows(U * j + u, u)
                        copy_ahead(j, u)

                later_groups(pool, group)

        @block.scalar
        def _(act):
            def split_hi(dest):
                for n in range(2):
                    cs = slice(n * KC // 2, (n + 1) * KC // 2)
                    nc.scalar.copy(dest(cs), wraw[:, cs, :]).then_inc(s_whi, 1)

            def distances(g):
                if not (isinstance(g, int) and g == 0):
                    act.wait_ge(s_hotd, g)
                for k in range(DEEP):
                    last = nc.scalar.activation(distance[:, k, :], iota_h[0:EP, 1:P + 1], ACT.Abs,
                                                bias=dp1_f[:, bass.ds(g * DEEP + k, 1)], scale=-1.0)
                last.then_inc(s_dist, 1)

            def in_block_onehots(g, half):
                act.wait_ge(s_dist, g + 1)
                nc.scalar.activation(oh_d[:, half, :, :], distance[:, :, :], ACT.Relu,
                                     bias=ones[0:EP, 0:1], scale=-1.0).then_inc(s_hotd, 1)

            act.wait_ge(s_dp1, 1)
            distances(0)
            act.wait_ge(s_wload, 16)
            split_hi(lambda cs: wr[:, 0, 0, cs, :])
            act.wait_ge(s_stats, 1)
            nc.scalar.activation(nrm[:, 0, :], nrm[:, 1, :], ACT.Sqrt).then_inc(s_std, 1)
            act.wait_ge(s_norm, 1)
            act.wait_ge(s_x, 16)

            def dense_hi(b, u):
                act.wait_ge(s_dT, b + 1)
                nc.scalar.copy(ahi[u][:, :, 0:ND], tview(0, ND)).then_inc(s_dhi, 1)

            def block_h(b):
                if not first_pair(b):
                    act.wait_ge(s_dT, b)
                    act.wait_ge(s_hst, 16 * b)
                nc.scalar.activation(rows[0][0:ND, :].unsqueeze(1), xt[:, bass.ds(b, 1), :], ACT.Relu,
                                     bias=nrm[:, 2, bass.ds(b, 1)],
                                     scale=nrm[:, 1, bass.ds(b, 1)]).then_inc(s_h, 1)
                act.wait_ge(s_h, b + 1)
                act.dma_start(h_dram[bass.ds(b * ND, ND), :], rows[0][0:ND, :]).then_inc(s_hst, 16)

            def root_out(b, bank):
                act.wait_ge(s_dprod, b + 1)
                nc.scalar.activation(acc[:, bass.ds(b, 1), :].rearrange("p o (h n) -> p (o h) n", h=2),
                                     product_view(bank, ND), ACT.Copy).then_inc(s_dev, 1)

            for b in range(EARLY):
                block_h(b)
                dense_hi(b, b)
            for b in range(EARLY):
                root_out(b, psT[1])

            def second_half(b):
                k = b - EARLY
                dense_hi(b, 0)
                if not (isinstance(k, int) and k == 0):
                    act.wait_ge(s_tab, k * COLS)
                distances(2 * k + 1)
                in_block_onehots(2 * k + 1, 1)

            def first_half(b):
                k = b - EARLY
                block_h(b)
                act.wait_ge(s_tab, k * COLS - DEEP)
                distances(2 * k)
                in_block_onehots(2 * k, 0)
                root_out(b - 1, psY[0])

            block_h(EARLY)
            act.wait_ge(s_pos, 1)
            in_block_onehots(0, 0)
            second_half(EARLY)
            with act.Fori(EARLY + 1, NB) as b:
                first_half(b)
                second_half(b)
            root_out(NB - 1, psY[0])
            act.wait_ge(s_wload, 32)
            act.wait_ge(s_tab, ET)
            split_hi(lambda cs: wr[:, 1, 0, cs, :])
            act.wait_ge(s_ctrl, 1)

            def tile_hi(t, u):
                act.wait_ge(s_T, t + 1)
                nc.scalar.copy(ahi[u][:, :, :], tview(0, P)).then_inc(s_hi, 1)

            def split_next_hi(t, very_first):
                rel, slot, first = layer_of(act, t)
                with act.If(first == 1):
                    if not very_first:
                        act.wait_ge(s_prod, t)
                    act.wait_ge(s_wload, rel * 16 + 48)
                    split_hi(lambda cs: wr[:, bass.ds(1 - slot, 1), 0, cs, :].rearrange("p o c n -> p (o c) n"))

            def tile_out(t, u, j):
                act.wait_ge(s_prod, t + 1)
                act.wait_ge(s_invg[u], 16 * j + 16)
                if not first_pair(j):
                    act.wait_ge(s_yst[u], 16 * j)
                nc.scalar.activation(halves(ysb[u][:, :]), yview(u, P), ACT.Copy,
                                     scale=invbuf[u][:, 0:1]).then_inc(s_evac, 1)
                act.wait_ge(s_evac, t + 1)
                act.dma_start(msg_dram[bass.ds(t * P, P), :], ysb[u][:, :]).then_inc(s_yst[u], 16)

            def pair(j):
                for u in range(2):
                    if not (first_pair(j) and u == 0):
                        act.wait_ge(s_prod, 2 * j + u)
                    tile_hi(2 * j + (u + 1), 1 - u)
                    split_next_hi(2 * j + u, first_pair(j) and u == 0)
                    tile_out(2 * j + u, u, j)

            tile_hi(0, 0)
            act.wait_ge(s_inv, 1)
            act.dma_start(inv_dram.rearrange("(b d r) o -> d b (r o)", b=NB, r=R),
                          inv[:, :, :]).then_inc(s_invst, 16)
            act.wait_ge(s_deg, 1)
            nc.scalar.activation(deg[:, 1, :], deg[:, 0, :], ACT.Sqrt).then_inc(s_sdeg, 1)
            every_pair(act, pair)

            def gcn_out(b):
                act.wait_ge(s_dprod, NB + b + 1)
                nc.scalar.activation(halves(acc[:, b, :]), yview(b % 2, ND), ACT.Copy,
                                     scale=dinv[:, b:b + 1]).then_inc(s_xw, 1)

            for b in range(NB):
                act.wait_ge(s_dT, NB + b + 1)
                if b >= 2:
                    act.wait_ge(s_dprod, NB + b - 1)
                nc.scalar.copy(ahi[b % 2][:, :, 0:ND], tview(1, ND)).then_inc(s_dhi, 1)
                if b:
                    gcn_out(b - 1)
            gcn_out(NB - 1)
            act.wait_ge(s_xwst, 16 * NB)
            for b in range(NB):
                act.wait_ge(s_aa[1], tiles_to_end(act, b))
                act.sem_inc(s_passed)
                nc.scalar.mul(acc[:, b, :], xt[:, b, :], dinv[:, b:b + 1]).then_inc(s_fin, 1)

        @block.vector
        def _(dve):
            chain = [0]
            V = nc.vector

            def step(ins):
                chain[0] += 1
                ins.then_inc(s_dve, 1)
                dve.wait_ge(s_dve, chain[0])

            def inverse_sqrt(y, v, root, t):
                step(V.reciprocal(root, root))
                step(V.tensor_tensor(t, root, root, ALU.mult))
                step(V.scalar_tensor_tensor(t, t, -0.5, v, ALU.mult, ALU.mult))
                step(V.tensor_scalar(t, t, 1.5, None, ALU.add))
                step(V.tensor_tensor(y, root, t, ALU.mult))

            dve.wait_ge(s_iota, 2)
            V.tensor_copy(part_f[:, :], part_i[:, :])
            V.tensor_copy(iota_h[:, :], iota_i[:, :])
            V.memset(ones[:, :], 1.0)
            V.memset(c128[:, :], float(P))
            step(V.tensor_copy(iota_f[:, :], iota_i[:, 0:TW]))
            V.tensor_scalar(tri[:, :], iota_f[:, 0:P], part_f[:, 0:1], None, ALU.is_gt)
            V.tensor_scalar(mcol[:, 0:1], part_f[:, :], 1.0, None, ALU.is_ge)
            V.tensor_scalar(mcol[:, 1:2], part_f[:, :], float(R), None, ALU.is_lt)
            V.tensor_scalar(mcol[:, 2:3], part_f[:, :], float(R + 1), None, ALU.is_ge)
            V.tensor_scalar(mcol[:, 5:6], part_f[:, :], float(R), None, ALU.is_ge)
            step(V.tensor_scalar(ident[:, :], iota_f[:, 0:P], part_f[:, 0:1], None, ALU.is_equal))
            V.tensor_scalar(masks[:, 0, :], ones[0:G, :], mcol[0:G, 0:1], mcol[0:G, 1:2], ALU.mult, ALU.mult)
            V.tensor_scalar(masks[:, 1, :], ones[0:G, :], mcol[0:G, 1:2], None, ALU.mult)
            V.tensor_scalar(masks[:, 2, :], ones[0:G, :], mcol[0:G, 2:3], None, ALU.mult)
            step(V.tensor_scalar(upto[:, :], tri[0:G, R + 1:R + 1 + NB], mcol[0:G, 5:6], None, ALU.mult))

            def split_lo(dest, layer2):
                for n in range(2):
                    cs = slice(n * KC // 2, (n + 1) * KC // 2)
                    dve.wait_ge(s_whi, layer2 + (n + 1))
                    if not isinstance(layer2, int):
                        dve.sem_inc(s_passed)
                    V.tensor_tensor(dest(1, cs), wraw[:, cs, :], dest(0, cs).bitcast(f32),
                                    ALU.subtract).then_inc(s_wlo, 1)

            def edges_to_float():
                dve.wait_ge(s_edges, 48)
                V.tensor_copy(src_f[:, :], edges_i[:, 0, :])
                V.tensor_copy(dst_f[:, :], edges_i[:, 1, :])
                step(V.tensor_copy(rel_f[:, :], edges_i[:, 2, :]))

            def node_block():
                step(V.tensor_scalar(pos_i[:, 0, :], dst_f[:, :], float(RECIPROCAL), None, ALU.mult))
                step(V.tensor_scalar(pos_i[:, 0, :], pos_i[:, 0, :], 20, None, ALU.arith_shift_right))
                step(V.tensor_copy(blk_f[:, :], pos_i[:, 0, :]))
                step(V.scalar_tensor_tensor(dp1_f[:, :], blk_f[:, :], -float(ND), dst_f[:, :],
                                            ALU.mult, ALU.add))
                V.scalar_tensor_tensor(cell_f[:, :], blk_f[:, :], float(R), rel_f[:, :], ALU.mult, ALU.add)
                step(V.tensor_scalar(dp1_f[:, :], dp1_f[:, :], 1.0, None, ALU.add))
                step(V.tensor_copy(edge_v[:, 2, :], src_f[:, :]))
                V.scalar_tensor_tensor(src_f[:, :], src_f[:, :], 2048.0, dst_f[:, :],
                                       ALU.mult, ALU.add).then_inc(s_dp1, 1)

            def dense_lo(b):
                dve.wait_ge(s_dhi, b + 1)
                u = b if isinstance(b, int) and b < EARLY else 0
                V.tensor_tensor(alo[u][:, :, 0:ND], tview(0, ND), ahi[u][:, :, 0:ND].bitcast(f32),
                                ALU.subtract).then_inc(s_dlo, 1)

            def relation_onehot():
                step(V.tensor_tensor(hot[:, 0:R, :], rel_f[:, :].unsqueeze(1).broadcast_to((EP, R, ET)),
                                     iota_f[0:EP, 0:R].unsqueeze(2).broadcast_to((EP, R, ET)), ALU.is_equal))

            def block_onehot():
                step(V.tensor_tensor(hot[:, R:G, :], blk_f[:, :].unsqueeze(1).broadcast_to((EP, NB, ET)),
                                     iota_f[0:EP, 0:NB].unsqueeze(2).broadcast_to((EP, NB, ET)), ALU.is_equal))

            def totals():
                part, width = hot, ET
                part3 = scan[:, :].rearrange("p (g t) -> p g t", g=G)
                while width % 2 == 0 and width > ET // 8:
                    width //= 2
                    step(V.tensor_tensor(part3[:, :, 0:width], part[:, :, 0:width],
                                         part[:, :, width:2 * width], ALU.add))
                    part = part3
                step(V.tensor_reduce(tot[:, :], part3[:, :, 0:width], AX.X, ALU.add))
                step(V.tensor_tensor_scan(tots[:, :], tot[:, :], tot[:, :], 0.0, ALU.add, ALU.max))

            edges_to_float()
            node_block()
            relation_onehot()
            block_onehot()
            totals()
            V.tensor_copy(tri_t[:, :], tri[0:G, 0:G]).then_inc(s_sm_in, 1)

            dve.wait_ge(s_x, 16)
            for b in range(NB):
                V.bn_stats(stats[:, 0, :], xt[:, b, 0:HALF])
                step(V.bn_stats(stats[:, 1, :], xt[:, b, HALF:D]))
                step(V.bn_aggr(mv[:, b, :], stats[:, :, :].rearrange("p a b -> p (a b)")))
            V.tensor_scalar(nrm[:, 1, :], mv[:, :, 1], EPS, None, ALU.add).then_inc(s_stats, 1)
            dve.wait_ge(s_std, 1)
            inverse_sqrt(nrm[:, 1, :], nrm[:, 1, :], nrm[:, 0, :], nrm[:, 2, :])
            V.scalar_tensor_tensor(nrm[:, 2, :], mv[:, :, 0], -1.0, nrm[:, 1, :],
                                   ALU.mult, ALU.mult).then_inc(s_norm, 1)

            dve.wait_ge(s_sm, 1)
            step(V.tensor_scalar(ncol[:, 0:1], psY[0][0:G, 0:1], float(P - 1), None, ALU.add))
            step(V.tensor_copy(ncol_i[:, 0:1], ncol[:, 0:1]))
            step(V.tensor_scalar(ncol_i[:, 1:2], ncol_i[:, 0:1], 7, None, ALU.arith_shift_right))
            step(V.tensor_copy(ncol[:, 1:2], ncol_i[:, 1:2]))
            step(V.tensor_scalar(ncol[:, 2:3], ncol[:, 1:2], mcol[0:G, 1:2], None, ALU.max))
            step(V.tensor_scalar(tri_t[:, 0:R], tri_t[:, 0:R], ncol[:, 2:3], None, ALU.mult))
            step(V.tensor_scalar(tri_t[:, R:G], tri_t[:, R:G], ncol[:, 2:3], masks[:, 2, 0:1],
                                 ALU.mult, ALU.mult))
            step(V.tensor_scalar(mcol[0:G, 3:4], part_f[0:G, :], float(R), None, ALU.is_equal))
            step(V.tensor_scalar(mcol[0:G, 4:5], ncol[:, 2:3], mcol[0:G, 3:4], None, ALU.mult))
            V.scalar_tensor_tensor(tri_t[:, R:G], tri[0:G, R:G], mcol[0:G, 4:5], tri_t[:, R:G],
                                   ALU.mult, ALU.add).then_inc(s_sm_in, 1)
            dve.wait_ge(s_sm, 2)
            step(V.tensor_tensor(delta[:, :], psY[1][0:EP, 8:8 + G], tots[:, :], ALU.subtract))
            step(V.tensor_tensor(delta[:, :], delta[:, :], tot[:, :], ALU.add))
            step(V.tensor_copy(savec[:, :], hot[:, :, 0]))
            V.tensor_tensor(hot[:, 0:1, 0], savec[:, 0:1], delta[:, 0:1], ALU.add)
            step(V.tensor_tensor(hot[:, 1:G, 0], savec[:, 1:G], delta[:, 1:G], ALU.add))
            step(V.tensor_tensor(hot[:, 1:G, 0], hot[:, 1:G, 0], delta[:, 0:G - 1], ALU.subtract))
            hot2 = hot[:, :, :].rearrange("p g t -> p (g t)")
            dense_lo(0)
            step(V.tensor_tensor_scan(scan[:, :], hot2, hot2, 0.0, ALU.add, ALU.bypass))
            step(V.tensor_copy(hot[:, :, 0], savec[:, :]))
            step(V.tensor_tensor(scan[:, :], scan[:, :], hot2, ALU.mult))
            dense_lo(1)
            scan3 = scan[:, :].rearrange("p (g t) -> p g t", g=G)

            def sum_groups(at, n, out):
                odd = []
                while n > 1:
                    if n % 2:
                        odd.append(at + n - 1)
                    n //= 2
                    step(V.tensor_tensor(scan3[:, at:at + n, :], scan3[:, at:at + n, :],
                                         scan3[:, at + n:at + 2 * n, :], ALU.add))
                assert len(odd) == 1
                step(V.tensor_tensor(out, scan3[:, at, :], scan3[:, odd[0], :], ALU.add))

            sum_groups(0, R, pos_f[:, 0, :])
            sum_groups(R, NB, pos_f[:, 1, :])
            step(V.tensor_scalar(pos_i[:, :, :], pos_f[:, :, :], -1.0, None, ALU.add))
            step(V.tensor_scalar(lo_i, pos_i[:, :, :], P - 1, None, ALU.bitwise_and))
            step(V.tensor_scalar(pos_i[:, :, :], pos_i[:, :, :], 7, None, ALU.arith_shift_right))
            V.tensor_copy(lo_f[:, :, :], lo_i).then_inc(s_pos, 1)
            step(V.tensor_copy(hi_f[:, :, :], pos_i[:, :, :]))
            step(V.tensor_scalar(pos_i[:, 1, :], lo_i[:, 0, :], 15, None, ALU.bitwise_and))
            step(V.tensor_copy(pos_f[:, 1, :], pos_i[:, 1, :]))
            step(V.scalar_tensor_tensor(edge_v[:, 1, :], pos_f[:, 1, :], float(P), dp1_f[:, :],
                                        ALU.mult, ALU.add))
            step(V.tensor_tensor(pos_f[:, 0, :], lo_f[:, 0, :], pos_f[:, 1, :], ALU.subtract))
            step(V.tensor_scalar(pos_f[:, 0, :], pos_f[:, 0, :], 1.0 / 16, None, ALU.mult))
            step(V.scalar_tensor_tensor(edge_v[:, 0, :], hi_f[:, 0, :], 8.0, pos_f[:, 0, :],
                                        ALU.mult, ALU.add))
            dve.wait_ge(s_sm, 3)
            step(V.tensor_copy(ncol[:, 3:4], psY[1][0:G, BANK:BANK + 1]))
            V.tensor_scalar(cmpt[:, 0, :], iota_f[0:G, :], ncol[:, 3:4], None, ALU.is_ge)
            V.tensor_scalar(cmpt[:, 1, :], iota_f[0:G, :], ncol[:, 3:4], None,
                            ALU.is_equal).then_inc(s_sm_in, 1)
            def onehots(c, u):
                def col(a):
                    return a[:, bass.ds(c, 1)]

                V.tensor_scalar(oh_lo1[u][:, :], iota_f[0:EP, 0:P], col(lo_f[:, 0, :]), None, ALU.is_equal)
                V.tensor_scalar(oh_m1[u][:, :], iota_f[0:EP, 0:MSG_TILES], col(hi_f[:, 0, :]),
                                col(src_f[:, :]), ALU.is_equal, ALU.mult)
                V.tensor_scalar(oh_c[u][:, :], iota_h[0:EP, :], col(cell_f[:, :]), None,
                                ALU.is_equal).then_inc(s_hot, 1)

            AHEAD = 3
            for c in range(AHEAD):
                onehots(c, c)
            dve.wait_ge(s_sm, 9)
            V.tensor_copy(rel_t[:, :], psY[0][:, 64:64 + TW])
            V.tensor_copy(sums[0:1, 0, 0:TW], psY[0][0:1, BANK:BANK + TW])
            V.tensor_copy(sums[0:1, 1, :], psY[1][0:1, BANK:BANK + TW + 2 + NB]).then_inc(s_sums, 1)

            def dst_onehots(c, u):
                def col(a):
                    return a[:, bass.ds(c, 1)]

                V.tensor_scalar(oh_lo2[u][:, :], iota_h[0:EP, 0:P], col(lo_f[:, 1, :]), None, ALU.is_equal)
                for n in range(3):
                    last = V.tensor_scalar(oh_m2[u][:, n, :], iota_h[0:EP, 0:AGG_TILES], col(hi_f[:, 1, :]),
                                           col(edge_v[:, n, :]), ALU.is_equal, ALU.mult)
                last.then_inc(s_hot2, 1)

            def root_block(b, peeled):
                for i in range(COLS):
                    c = (b - EARLY) * COLS + i
                    if not (peeled and i < DEEP):
                        dve.wait_ge(s_tab, (b - EARLY) * COLS + (i - DEEP + 1))
                    if not (peeled and i < AHEAD):
                        onehots(c, i % DEEP)
                    if i == 7:
                        dense_lo(b)

            root_block(EARLY, True)
            with dve.Fori(EARLY + 1, NB) as b:
                root_block(b, False)

            V.tensor_copy(ctrl[0:1, BLK, :], sums[0:1, 1, 0:TW])
            step(V.tensor_scalar(word[0:1, 0, :], rel_t[0:1, :], 1.0, None, ALU.add))
            step(V.tensor_scalar(word[0:1, 1, :], word[0:1, 0, :], 1, 1, ALU.bitwise_and, ALU.logical_shift_left))
            step(V.tensor_tensor(word[0:1, 2, :], sums[0:1, 0, 0:TW], word[0:1, 1, :], ALU.add))
            V.scalar_tensor_tensor(ctrl[0:1, LAYER, :], rel_t[0:1, :], 4.0, word[0:1, 2, :],
                                   ALU.mult, ALU.add)
            step(V.tensor_scalar(ctrl[0:1, TOTAL, 0:1], sums[0:1, 1, TW:TW + 1], 1.0,
                                 float(2 * SURE_PAIRS), ALU.add, ALU.max))
            step(V.tensor_scalar(ctrl[0:1, TOTAL, 0:1], ctrl[0:1, TOTAL, 0:1], 1, 1,
                                 ALU.arith_shift_right, ALU.logical_shift_left))
            V.tensor_scalar(ctrl[0:1, END, 0:NB], sums[0:1, 1, TW + 2:TW + 2 + NB], 1.0, None,
                            ALU.max)
            step(V.tensor_scalar(tots[0:1, 0:AGG_GROUPS], iota_f[0:1, 0:AGG_GROUPS], float(U), None, ALU.mult))
            step(V.tensor_scalar(tots[0:1, 0:AGG_GROUPS], tots[0:1, 0:AGG_GROUPS], sums[0:1, 1, TW + 1:TW + 2],
                                 None, ALU.is_lt))
            step(V.tensor_reduce(savec[0:1, 1:2], tots[0:1, 0:AGG_GROUPS], AX.X, ALU.add))
            V.tensor_scalar(ctrl[0:1, TOTAL, 1:2], savec[0:1, 1:2], float(U), float(U * SURE_GROUPS),
                            ALU.mult, ALU.max).then_inc(s_ctrl, 1)

            for a in (idx_src, idx_cell, idx_msg, idx_xw):
                V.memset(a[:, :], 0)
            step(V.memset(dloc[:, :], -1.0))
            dve.wait_ge(s_tab, ET)
            M = MSG_TILES
            step(V.tensor_copy(word[:, 0, 0:M], psT[1][:, 0:M]))
            V.tensor_scalar(idx_src[:, 0:M], word[:, 0, 0:M], 11, None, ALU.arith_shift_right).then_inc(s_tables, 1)
            step(V.tensor_scalar(word[:, 1, 0:M], word[:, 0, 0:M], 2047, None, ALU.bitwise_and))
            V.scalar_tensor_tensor(idx_cell[:, 0:M], word[:, 1, 0:M], float(R), rel_t[:, 0:M],
                                   ALU.mult, ALU.add)
            split_lo(lambda part, cs: wr[:, 1, part, cs, :], 2)

            def tile_lo(t, u):
                dve.wait_ge(s_hi, t + 1)
                V.tensor_tensor(alo[u][:, :, :], tview(0, P), ahi[u][:, :, :].bitcast(f32),
                                ALU.subtract).then_inc(s_lo, 1)

            def split_next_lo(t):
                rel, slot, first = layer_of(dve, t)
                with dve.If(first == 1):
                    split_lo(lambda part, cs: wr[:, bass.ds(1 - slot, 1), part, cs, :]
                             .rearrange("p o c n -> p (o c) n"), 2 * rel + 4)

            columns = [True]

            def pair(j):
                for u in range(2):
                    tile_lo(2 * j + (u + 1), 1 - u)
                    if columns[0]:
                        if not first_pair(j):
                            dve.wait_ge(s_tab2, 2 * j + (u - 1))
                        dst_onehots(2 * j + u, u)
                    split_next_lo(2 * j + u)

            def unpack():
                columns[0] = False
                A = AGG_TILES
                dve.wait_ge(s_tab2, ET)
                V.tensor_copy(idx_xw[:, 0:A], psT[1][:, 2 * A:3 * A])
                V.tensor_copy(word[:, 0, 0:A], psT[1][:, 0:A])
                step(V.tensor_copy(word[:, 1, 0:A], psT[1][:, A:2 * A]))
                step(V.tensor_scalar(word[:, 2, 0:A], word[:, 1, 0:A], 7, None, ALU.arith_shift_right))
                V.scalar_tensor_tensor(idx_msg[:, 0:A], word[:, 0, 0:A], 16.0, word[:, 2, 0:A],
                                       ALU.mult, ALU.add)
                step(V.tensor_scalar(word[:, 3, 0:A], word[:, 1, 0:A], P - 1, None, ALU.bitwise_and))
                V.tensor_scalar(dloc[:, 0:A], word[:, 3, 0:A], -1.0, None, ALU.add).then_inc(s_tables2, 1)
                dve.wait_ge(s_sdeg, 1)
                V.tensor_copy(degree[:, :], deg[:, 0, :])
                inverse_sqrt(dinv[:, :], deg[:, 0, :], deg[:, 1, :], deg[:, 2, :])

            tile_lo(0, 0)
            step(V.tensor_copy(cnt[:, :, :], psT[1][0:ND, BANK:BANK + NB * R].rearrange("p (b r) -> p b r", b=NB)))
            V.tensor_reduce(deg[:, 0, :], cnt[:, :, :], AX.X, ALU.add)
            step(V.tensor_scalar(inv[:, :, :], cnt[:, :, :], 1.0, None, ALU.max))
            V.tensor_scalar(deg[:, 0, :], deg[:, 0, :], 1.0, None, ALU.add).then_inc(s_deg, 1)
            V.reciprocal(inv[:, :, :], inv[:, :, :]).then_inc(s_inv, 1)

            every_pair(dve, pair, unpack)

            def aggregate(ph, into):
                def select(w, u):
                    V.tensor_scalar(selector[u][:, :], iota_f[:, 0:P], dloc[:, bass.ds(w, 1)], None,
                                    ALU.is_equal).then_inc(s_sel[ph], 1)

                def add(w, u):
                    blk = dve.value_load(ctrl[0:1, BLK, bass.ds(w, 1)], min_val=0, max_val=NB - 1)
                    dve.wait_ge(s_ap[ph], w + 1)
                    if not (isinstance(w, int) and w == 0):
                        dve.wait_ge(s_aa[ph], w)
                    sums = into[:, bass.ds(blk, 1), :].rearrange("p o (h n) -> p (o h) n", h=2)
                    V.tensor_tensor(sums, agg_psum(u), sums, ALU.add).then_inc(s_aa[ph], 1)

                select(0, 0)
                select(1, 1)
                for w in range(U):
                    select(w + 2, (w + 2) % 3)
                    add(w, w % 3)

                def group(j):
                    for u in range(U):
                        select(U * j + (u + 2), (u + 2) % 3)
                        add(U * j + u, u % 3)

                later_groups(dve, group)

            dve.wait_ge(s_rb, NB)
            dve.wait_ge(s_fill, 16 * NB)
            aggregate(0, acc)
            step(V.tensor_tensor(deg[:, 1, :], degree[:, :], dinv[:, :], ALU.mult))

            def sums_start(b):
                dve.wait_ge(s_xw, b + 1)
                V.scalar_tensor_tensor(xt[:, b, :], xt[:, b, :], deg[:, 1, b:b + 1], acc[:, b, :],
                                       ALU.mult, ALU.add).then_inc(s_self, 1)

            dve.wait_ge(s_xb, NB)
            for b in range(NB):
                dve.wait_ge(s_dhi, NB + b + 1)
                V.tensor_tensor(alo[b % 2][:, :, 0:ND], tview(1, ND), ahi[b % 2][:, :, 0:ND].bitcast(f32),
                                ALU.subtract).then_inc(s_dlo, 1)
                if b >= 2:
                    sums_start(b - 2)
            sums_start(NB - 2)
            sums_start(NB - 1)
            dve.wait_ge(s_self, NB)
            aggregate(1, xt)

        @block.tensor
        def _(pe):
            mm = nc.tensor.matmul

            def transpose_block(source, u):
                for c in range(KC):
                    last = nc.tensor.transpose(tview(u, ND)[:, c, :], source[:, c * P:(c + 1) * P],
                                               ident[0:ND, 0:ND])
                last.then_inc(s_dT, 1)

            def product(a, m, w_hi, w_lo, bank, hs=(0, 1)):
                for h in hs:
                    o = bank[0:m, h * BANK:h * BANK + HALF]
                    for c in range(KC):
                        hi, lo = ahi[a][:, c, 0:m], alo[a][:, c, 0:m]
                        mm(o, hi, w_hi(c, h), start=(c == 0), stop=False)
                        mm(o, hi, w_lo(c, h), start=False, stop=False)
                        last = mm(o, lo, w_hi(c, h), start=False, stop=(c == KC - 1))
                return last

            def static_w(slot, part):
                return lambda c, h: wr[:, slot, part, c, h * HALF:(h + 1) * HALF]

            pe.wait_ge(s_sm_in, 1)
            mm(psY[0][0:G, 0:1], tot[:, :], ones[0:EP, 0:1], start=True, stop=True).then_inc(s_sm, 1)
            pe.wait_ge(s_sm_in, 2)
            o = psY[1][0:EP, 8:8 + G]
            mm(o, tri[0:EP, 0:EP], tot[:, :], start=True, stop=False)
            mm(o, c128[0:G, 0:EP], tri_t[:, :], start=False, stop=True).then_inc(s_sm, 1)
            mm(psY[1][0:G, BANK:BANK + 1], tri_t[:, :], ones[0:G, 0:1], start=True, stop=True).then_inc(s_sm, 1)
            for b in range(EARLY):
                pe.wait_ge(s_h, b + 1)
                transpose_block(rows[0][0:ND, :], 0)
                pe.wait_ge(s_dlo, b + 1)
                if b == 0:
                    pe.wait_ge(s_wlo, 2)
                else:
                    pe.wait_ge(s_dev, b)
                product(b, ND, static_w(0, 0), static_w(0, 1), psT[1]).then_inc(s_dprod, 1)
            pe.wait_ge(s_sm_in, 3)
            mm(psY[0][:, 64:64 + TW], masks[:, 0, :], cmpt[:, 0, :], start=True, stop=True).then_inc(s_sm, 1)
            mm(psY[0][:, BANK:BANK + TW], masks[:, 1, :], cmpt[:, 1, :], start=True, stop=True).then_inc(s_sm, 1)
            mm(psY[1][:, BANK:BANK + TW], masks[:, 2, :], cmpt[:, 0, :], start=True, stop=True).then_inc(s_sm, 1)
            mm(psY[1][:, BANK + TW:BANK + TW + 1], masks[:, 1, :], ncol[:, 2:3], start=True,
               stop=True).then_inc(s_sm, 1)
            mm(psY[1][0:1, BANK + TW + 1:BANK + TW + 2], mcol[0:G, 5:6], ncol[:, 2:3], start=True,
               stop=True).then_inc(s_sm, 1)
            mm(psY[1][0:1, BANK + TW + 2:BANK + TW + 2 + NB], ncol[:, 2:3], upto[:, :], start=True,
               stop=True).then_inc(s_sm, 1)

            def move(k, i, start):
                pe.wait_ge(s_hot, k * COLS + (i + 1))
                u = i % DEEP
                if u == 0:
                    pe.wait_ge(s_hotd, 2 * k + (i // DEEP + 1))
                mm(psT[1][:, 0:MSG_TILES], oh_lo1[u][:, :], oh_m1[u][:, :], start=start, stop=False,
                   skip_group_check=True)
                mm(psT[1][:, BANK:BANK + NB * R], oh_d[:, i // DEEP, u, :], oh_c[u][:, :], start=start,
                   stop=False, skip_group_check=True).then_inc(s_tab, 1)

            def root_block(b, peeled):
                pe.wait_ge(s_h, b + 1)
                pe.wait_ge(s_dlo, b)
                transpose_block(rows[0][0:ND, :], 0)
                for i in range(COLS):
                    move(b - EARLY, i, peeled and i == 0)
                    if i == 6:
                        if peeled:
                            pe.wait_ge(s_sums, 1)
                        pe.wait_ge(s_dlo, b + 1)
                        pe.wait_ge(s_dev, b)
                        product(0, ND, static_w(0, 0), static_w(0, 1), psY[0], (0,))
                    if i == 12:
                        product(0, ND, static_w(0, 0), static_w(0, 1), psY[0], (1,)).then_inc(s_dprod, 1)

            pe.wait_ge(s_dev, EARLY)
            root_block(EARLY, True)
            with pe.Fori(EARLY + 1, NB) as b:
                root_block(b, False)

            def dst_move(c, u, start, stop):
                pe.wait_ge(s_hot2, c + 1)
                mm(psT[1][:, 0:3 * AGG_TILES], oh_lo2[u][:, :],
                   oh_m2[u][:, :, :].rearrange("p v t -> p (v t)"), start=start, stop=stop,
                   skip_group_check=True).then_inc(s_tab2, 1)

            def tile_transpose(t, u, count):
                pe.wait_ge(s_rows[u], 16 * count)
                for c in range(KC):
                    last = nc.tensor.transpose(tview(0, P)[:, c, :], rows[u][:, c * P:(c + 1) * P], ident[:, :])
                last.then_inc(s_T, 1)

            def tile_product(t, u):
                rel, slot, _ = layer_of(pe, t)
                pe.wait_ge(s_wlo, 2 * rel + 4)
                part = [wr[:, bass.ds(slot, 1), k, :, :].rearrange("p o c n -> p (o c) n") for k in range(2)]
                product(u, P, lambda c, h: part[0][:, c, h * HALF:(h + 1) * HALF],
                        lambda c, h: part[1][:, c, h * HALF:(h + 1) * HALF], psY[u]).then_inc(s_prod, 1)

            columns = [True]

            def pair(j):
                for u in range(2):
                    pe.wait_ge(s_lo, 2 * j + (u + 1))
                    tile_transpose(2 * j + (u + 1), 1 - u, j + (1 + u))
                    if not first_pair(j):
                        pe.wait_ge(s_evac, 2 * j + (u - 1))
                    tile_product(2 * j + u, u)
                    if columns[0]:
                        dst_move(2 * j + u, u, first_pair(j) and u == 0, False)

            def columns_done():
                columns[0] = False

            pe.wait_ge(s_tables, 1)
            tile_transpose(0, 0, 1)
            every_pair(pe, pair, columns_done)
            pe.wait_ge(s_evac, tiles_done(pe))

            def aggregate(ph):
                def sums(w, u, count):
                    pe.wait_ge(s_sel[ph], w + 1)
                    pe.wait_ge(s_g6[ph][u], 16 * count)
                    for h in range(2):
                        last = mm(agg_psum(u % 3)[:, h, :], selector[u % 3][:, 0:ND],
                                  rows6[:, u, :][:, h * HALF:(h + 1) * HALF], start=True, stop=True)
                    last.then_inc(s_ap[ph], 1)

                for u in range(U):
                    if u >= 3:
                        pe.wait_ge(s_aa[ph], u - 2)
                    sums(u, u, 1)

                def group(j):
                    for u in range(U):
                        pe.wait_ge(s_aa[ph], U * j + (u - 2))
                        sums(U * j + u, u, j + 1)

                later_groups(pe, group)

            aggregate(0)

            slot = (R + 1) % 2
            pe.wait_ge(s_aa[0], tiles_to_end(pe, 0))
            transpose_block(acc[:, 0, :], 1)
            pe.wait_ge(s_aa[0], dst_tiles_done(pe))
            for b in range(NB):
                pe.wait_ge(s_dlo, NB + b + 1)
                if b < NB - 1:
                    transpose_block(acc[:, b + 1, :], 1)
                if b >= 2:
                    pe.wait_ge(s_xw, b - 1)
                product(b % 2, ND, static_w(slot, 0), static_w(slot, 1), psY[b % 2]).then_inc(s_dprod, 1)
            pe.wait_ge(s_xw, NB)
            aggregate(1)


_INS = ['x', 'src', 'dst', 'edge_type_34', 'L0_gnn_W_rel', 'L0_gnn_W_root', 'L0_gnn_b_rgcn', 'L0_gnn_W_gcn',
        'L0_gnn_b_gcn']
_OUTS = [((1250, 768), 'float32')]


def kernel(**inputs):
    import numpy as _np
    import concourse.bacc as _bacc
    from concourse import mybir as _mybir
    from concourse.bass_utils import run_bass_kernel_spmd as _run

    nc = _bacc.Bacc("TRN2", target_bir_lowering=False, num_devices=1)
    arrays, args = {}, []
    for name in _INS:
        a = _np.ascontiguousarray(inputs[name])
        arrays[f"in_{name}_dram"] = a
        args.append(nc.dram_tensor(f"in_{name}_dram", a.shape, _mybir.dt.from_np(a.dtype), kind="ExternalInput").ap())
    for i, (shape, dtype) in enumerate(_OUTS):
        dt = _mybir.dt.from_np(_np.dtype(dtype))
        args.append(nc.dram_tensor(f"out_{i}_dram", shape, dt, kind="ExternalOutput").ap())
    relational_gnn_kernel(nc, *args)
    r = _run(nc, [arrays], core_ids=[0])
    got = tuple(r.results[0][f"out_{i}_dram"] for i in range(len(_OUTS)))
    return got[0]
```
